# Optimizing a Trainium2 kernel written in Bass

```python
import numpy as np
import jax
import jax.numpy as jnp

def _softmax(x, axis=-1):
    return jax.nn.softmax(x, axis=axis)

def _gelu(x):
    return jax.nn.gelu(x, approximate=True)

def _silu(x):
    return jax.nn.silu(x)

def _sigmoid(x):
    return jax.nn.sigmoid(x)

def _layernorm(x, axis=-1, eps=1e-05):
    m = jnp.mean(x, axis=axis, keepdims=True)
    v = jnp.var(x, axis=axis, keepdims=True)
    return (x - m) / jnp.sqrt(v + eps)

def _scatter_add(tgt, idx, src, axis=0):
    return tgt.at[idx].add(src)

def _segment_sum(src, seg, n):
    return jax.ops.segment_sum(src, seg, n)
kernel_name = 'mk_prb_d1_jaxref_r8_286d53'

def setup_inputs(seed: int=0):
    np.random.seed(seed)
    _w = jnp.asarray

    def _L0_attn_setup():
        import jax, jax.numpy as jnp
        import numpy as np
        HID, H, KV, D = (256, 16, 4, 128)
        ROPE_THETA = 10000.0
        GATE_NORM = 16.0

        def _rope_cos_sin(n, d, dtype=jnp.float32):
            inv_freq = 1.0 / ROPE_THETA ** (jnp.arange(0, d, 2, dtype=jnp.float32) / d)
            freqs = jnp.arange(n, dtype=jnp.float32)[:, None] * inv_freq[None, :]
            cos = jnp.cos(freqs).astype(dtype)[None, :, None, :]
            sin = jnp.sin(freqs).astype(dtype)[None, :, None, :]
            return (cos, sin)

        def _apply_rotary(x, cos, sin):
            x1, x2 = jnp.split(x, 2, axis=-1)
            return jnp.concatenate([x1 * cos - x2 * sin, x2 * cos + x1 * sin], axis=-1)

        def _forward(hidden_states, Wq, Wk, Wv, Wo):
            b, n, _ = hidden_states.shape
            groups = H // KV
            q = hidden_states @ Wq
            k = hidden_states @ Wk
            v = hidden_states @ Wv
            g = k
            q = q.reshape(b, n, H, D)
            k = k.reshape(b, n, KV, D)
            v = v.reshape(b, n, KV, D)
            g = g.reshape(b, n, KV, D)
            k = jnp.repeat(k, groups, axis=2)
            v = jnp.repeat(v, groups, axis=2)
            g = jnp.repeat(g, groups, axis=2)
            sq, sk, sv = (q, k, v)
            qs = jax.nn.softmax(q.astype(jnp.float32), axis=-1)
            ks = jax.nn.softmax(k.astype(jnp.float32), axis=-1)
            gl = jax.nn.log_sigmoid(g.astype(jnp.float32)) / GATE_NORM
            cos, sin = _rope_cos_sin(n, D)
            sq = _apply_rotary(sq, cos, sin)
            sk = _apply_rotary(sk, cos, sin)

            def step(S, inp):
                q_t, k_t, v_t, g_t = inp
                S = S * jnp.exp(g_t)[..., None] + k_t[..., None] * v_t[..., None, :]
                o_t = jnp.einsum('bhk,bhkv->bhv', q_t, S)
                return (S, o_t)
            xs = tuple((jnp.moveaxis(a, 1, 0) for a in (qs, ks, v, gl)))
            S0 = jnp.zeros((b, H, D, D), dtype=jnp.float32)
            _, o_gla = jax.lax.scan(step, S0, xs)
            o_gla = jnp.moveaxis(o_gla, 0, 1)
            scale = D ** (-0.5)
            scores = jnp.einsum('bqhd,bkhd->bhqk', sq, sk) * scale
            causal = jnp.tril(jnp.ones((n, n), dtype=bool))
            scores = jnp.where(causal[None, None], scores, jnp.finfo(scores.dtype).min)
            attn = jax.nn.softmax(scores, axis=-1)
            y = jnp.einsum('bhqk,bkhd->bqhd', attn, sv)
            o = 0.5 * y + 0.5 * o_gla
            o = o.reshape(b, n, H * D).astype(hidden_states.dtype)
            return o @ Wo
        key = jax.random.key(seed)
        k1, k2, k3, k4, k5 = jax.random.split(key, 5)
        s = 0.02
        return {'hidden_states': jax.random.normal(k1, (1, 256, HID), dtype=jnp.float32), 'Wq': jax.random.normal(k2, (HID, H * D), dtype=jnp.float32) * s, 'Wk': jax.random.normal(k3, (HID, KV * D), dtype=jnp.float32) * s, 'Wv': jax.random.normal(k4, (HID, KV * D), dtype=jnp.float32) * s, 'Wo': jax.random.normal(k5, (H * D, HID), dtype=jnp.float32) * s}
    _L0_attn_in = _L0_attn_setup()

    def _L0_ffn_setup():
        import jax, jax.numpy as jnp
        import numpy as np
        import math
        D_MODEL = 256
        D_FF = 1024
        NUM_EXPERTS = 8
        TOP_K = 2
        CAPACITY_FACTOR = 1.25
        BATCH, SEQ = (4, 256)

        def _moe_forward(x, Wg, w1, w2):
            B, T, d = x.shape
            S = B * T
            E, K = (NUM_EXPERTS, TOP_K)
            C = math.ceil(CAPACITY_FACTOR * S * K / E)
            xr = x.reshape(S, d)
            probs = jax.nn.softmax(xr @ Wg, axis=-1)
            gate_vals, expert_idx = jax.lax.top_k(probs, K)
            flat_e = expert_idx.reshape(-1)
            oh = jax.nn.one_hot(flat_e, E, dtype=jnp.int32)
            pos = jnp.sum((jnp.cumsum(oh, axis=0) - 1) * oh, axis=1)
            kept = pos < C
            i = jnp.arange(S * K)
            slot = i % K * S + i // K
            sentinel = S * K
            pos_w = jnp.where(kept, pos, C)
            dispatch_mask = jnp.full((E, C), sentinel, dtype=jnp.int32)
            dispatch_mask = dispatch_mask.at[flat_e, pos_w].set(slot.astype(jnp.int32), mode='drop')
            combine_weights = (gate_vals * kept.reshape(S, K)).T
            dispatched = xr[dispatch_mask.reshape(-1) % S].reshape(E, C, d)
            h = jax.nn.relu(jnp.einsum('ecd,edf->ecf', dispatched, w1))
            expert_out = jnp.einsum('ecf,efd->ecd', h, w2)
            rerouted = jnp.zeros((S * K + 1, d), dtype=expert_out.dtype)
            rerouted = rerouted.at[dispatch_mask.reshape(-1)].set(expert_out.reshape(-1, d))
            rerouted = rerouted[:-1].reshape(K, S, d)
            out = jnp.einsum('ks,ksm->sm', combine_weights, rerouted)
            return out.reshape(B, T, d)
        key = jax.random.key(seed)
        k1, k2, k3, k4 = jax.random.split(key, 4)
        x = jax.random.normal(k1, (BATCH, SEQ, D_MODEL), dtype=jnp.float32)
        Wg = jax.random.normal(k2, (D_MODEL, NUM_EXPERTS), dtype=jnp.float32) * 0.02
        w1 = jax.random.normal(k3, (NUM_EXPERTS, D_MODEL, D_FF), dtype=jnp.float32) * 0.02
        w2 = jax.random.normal(k4, (NUM_EXPERTS, D_FF, D_MODEL), dtype=jnp.float32) * 0.02
        return {'x': x, 'Wg': Wg, 'w1': w1, 'w2': w2}
    _L0_ffn_in = _L0_ffn_setup()
    _d = {'L0_attn_hidden_states': _L0_attn_in['hidden_states'], 'L0_attn_Wq': _L0_attn_in['Wq'], 'L0_attn_Wk': _L0_attn_in['Wk'], 'L0_attn_Wv': _L0_attn_in['Wv'], 'L0_attn_Wo': _L0_attn_in['Wo'], 'L0_ffn_Wg': _L0_ffn_in['Wg'], 'L0_ffn_w1': _L0_ffn_in['w1'], 'L0_ffn_w2': _L0_ffn_in['w2']}
    _x0 = _d['L0_attn_hidden_states']
    _d['L0_attn_hidden_states'] = jax.random.normal(jax.random.fold_in(jax.random.key(seed), 1), (2, 1024, 256), dtype=_x0.dtype)
    del _x0
    return _d

def reference(L0_attn_hidden_states, L0_attn_Wq, L0_attn_Wk, L0_attn_Wv, L0_attn_Wo, L0_ffn_Wg, L0_ffn_w1, L0_ffn_w2):

    def _L0_attn_ref(hidden_states, Wq, Wk, Wv, Wo):
        import jax, jax.numpy as jnp
        import numpy as np
        HID, H, KV, D = (256, 16, 4, 128)
        ROPE_THETA = 10000.0
        GATE_NORM = 16.0

        def _rope_cos_sin(n, d, dtype=jnp.float32):
            inv_freq = 1.0 / ROPE_THETA ** (jnp.arange(0, d, 2, dtype=jnp.float32) / d)
            freqs = jnp.arange(n, dtype=jnp.float32)[:, None] * inv_freq[None, :]
            cos = jnp.cos(freqs).astype(dtype)[None, :, None, :]
            sin = jnp.sin(freqs).astype(dtype)[None, :, None, :]
            return (cos, sin)

        def _apply_rotary(x, cos, sin):
            x1, x2 = jnp.split(x, 2, axis=-1)
            return jnp.concatenate([x1 * cos - x2 * sin, x2 * cos + x1 * sin], axis=-1)

        def _forward(hidden_states, Wq, Wk, Wv, Wo):
            b, n, _ = hidden_states.shape
            groups = H // KV
            q = hidden_states @ Wq
            k = hidden_states @ Wk
            v = hidden_states @ Wv
            g = k
            q = q.reshape(b, n, H, D)
            k = k.reshape(b, n, KV, D)
            v = v.reshape(b, n, KV, D)
            g = g.reshape(b, n, KV, D)
            k = jnp.repeat(k, groups, axis=2)
            v = jnp.repeat(v, groups, axis=2)
            g = jnp.repeat(g, groups, axis=2)
            sq, sk, sv = (q, k, v)
            qs = jax.nn.softmax(q.astype(jnp.float32), axis=-1)
            ks = jax.nn.softmax(k.astype(jnp.float32), axis=-1)
            gl = jax.nn.log_sigmoid(g.astype(jnp.float32)) / GATE_NORM
            cos, sin = _rope_cos_sin(n, D)
            sq = _apply_rotary(sq, cos, sin)
            sk = _apply_rotary(sk, cos, sin)

            def step(S, inp):
                q_t, k_t, v_t, g_t = inp
                S = S * jnp.exp(g_t)[..., None] + k_t[..., None] * v_t[..., None, :]
                o_t = jnp.einsum('bhk,bhkv->bhv', q_t, S)
                return (S, o_t)
            xs = tuple((jnp.moveaxis(a, 1, 0) for a in (qs, ks, v, gl)))
            S0 = jnp.zeros((b, H, D, D), dtype=jnp.float32)
            _, o_gla = jax.lax.scan(step, S0, xs)
            o_gla = jnp.moveaxis(o_gla, 0, 1)
            scale = D ** (-0.5)
            scores = jnp.einsum('bqhd,bkhd->bhqk', sq, sk) * scale
            causal = jnp.tril(jnp.ones((n, n), dtype=bool))
            scores = jnp.where(causal[None, None], scores, jnp.finfo(scores.dtype).min)
            attn = jax.nn.softmax(scores, axis=-1)
            y = jnp.einsum('bhqk,bkhd->bqhd', attn, sv)
            o = 0.5 * y + 0.5 * o_gla
            o = o.reshape(b, n, H * D).astype(hidden_states.dtype)
            return o @ Wo
        return _forward(hidden_states, Wq, Wk, Wv, Wo)

    def _L0_ffn_ref(x, Wg, w1, w2):
        import jax, jax.numpy as jnp
        import numpy as np
        import math
        D_MODEL = 256
        D_FF = 1024
        NUM_EXPERTS = 8
        TOP_K = 2
        CAPACITY_FACTOR = 1.25
        BATCH, SEQ = (4, 256)

        def _moe_forward(x, Wg, w1, w2):
            B, T, d = x.shape
            S = B * T
            E, K = (NUM_EXPERTS, TOP_K)
            C = math.ceil(CAPACITY_FACTOR * S * K / E)
            xr = x.reshape(S, d)
            probs = jax.nn.softmax(xr @ Wg, axis=-1)
            gate_vals, expert_idx = jax.lax.top_k(probs, K)
            flat_e = expert_idx.reshape(-1)
            oh = jax.nn.one_hot(flat_e, E, dtype=jnp.int32)
            pos = jnp.sum((jnp.cumsum(oh, axis=0) - 1) * oh, axis=1)
            kept = pos < C
            i = jnp.arange(S * K)
            slot = i % K * S + i // K
            sentinel = S * K
            pos_w = jnp.where(kept, pos, C)
            dispatch_mask = jnp.full((E, C), sentinel, dtype=jnp.int32)
            dispatch_mask = dispatch_mask.at[flat_e, pos_w].set(slot.astype(jnp.int32), mode='drop')
            combine_weights = (gate_vals * kept.reshape(S, K)).T
            dispatched = xr[dispatch_mask.reshape(-1) % S].reshape(E, C, d)
            h = jax.nn.relu(jnp.einsum('ecd,edf->ecf', dispatched, w1))
            expert_out = jnp.einsum('ecf,efd->ecd', h, w2)
            rerouted = jnp.zeros((S * K + 1, d), dtype=expert_out.dtype)
            rerouted = rerouted.at[dispatch_mask.reshape(-1)].set(expert_out.reshape(-1, d))
            rerouted = rerouted[:-1].reshape(K, S, d)
            out = jnp.einsum('ks,ksm->sm', combine_weights, rerouted)
            return out.reshape(B, T, d)
        return _moe_forward(x, Wg, w1, w2)
    x = L0_attn_hidden_states
    xn = _layernorm(x, axis=-1)
    x = x + _L0_attn_ref(xn, L0_attn_Wq, L0_attn_Wk, L0_attn_Wv, L0_attn_Wo) + _L0_ffn_ref(xn, L0_ffn_Wg, L0_ffn_w1, L0_ffn_w2)
    return x

_drawn_inputs = setup_inputs


def setup_inputs(seed=0):
    import zlib

    import numpy as np

    out = dict(_drawn_inputs(seed))
    spreads = {}
    factors = {'L0_attn_Wq': 8.0,
     'L0_attn_Wk': 8.0,
     'L0_attn_Wv': 4.053,
     'L0_attn_Wo': 3.926,
     'L0_ffn_Wg': 3.638,
     'L0_ffn_w1': 3.757,
     'L0_ffn_w2': 3.128}
    for name, (base, spread) in spreads.items():
        noise = np.random.default_rng([zlib.crc32(name.encode()), seed]).standard_normal(out[name].shape)
        drawn = base * np.exp(spread * noise) if base else spread * noise
        out[name] = jnp.asarray(drawn.astype(out[name].dtype))
    for name, factor in factors.items():
        out[name] = (out[name] * factor).astype(out[name].dtype)
    return out
```

```python
import numpy as np
import concourse.bass as bass
from concourse import mybir
from contextlib import ExitStack

F32 = mybir.dt.float32
BF16 = mybir.dt.bfloat16
I32 = mybir.dt.int32
ALU = mybir.AluOpType
ACT = mybir.ActivationFunctionType
AX = mybir.AxisListType

P = 128
B, N, HID = 2, 1024, 256
H, KV, D = 16, 4, 128
GROUPS = H // KV
HD = GROUPS * D
KC = HID // P
CH = N // P
TILES = B * CH
TOK = B * N
QKV = HD + 2 * D
FF, E, TOP_K = 1024, 8, 2
FC = FF // P
CAP = -(-5 * TOK * TOP_K // (4 * E))
ST = CAP // P
SLOTS = E * CAP
HALF = CAP // 2
EPS = 1e-5
GATE_NORM = 16.0
SCALE = float(D) ** -0.5
BIG = 1e30
MID = D // 2 - 1
START = 1
EXP_AND_LN = 6
FAR = 8192.0

C_ID, C_CUM, C_STRICT, C_ONES, C_MIN = (P * i for i in range(5))
C_COS = 5 * P
C_SIN = C_COS + CH * (D // 2)
C_NSIN = C_SIN + CH * (D // 2)
C_RANK = C_NSIN + CH * (D // 2)
C_BASE = C_RANK + E
C_ALL = C_BASE + E


def constants():
    j, i = np.arange(P)[:, None], np.arange(P)[None, :]
    c = np.zeros((P, C_ALL), np.float32)
    c[:, C_ID:C_ID + P] = j == i
    c[:, C_CUM:C_CUM + P] = (j <= i) / GATE_NORM
    c[:, C_STRICT:C_STRICT + P] = j < i
    c[:, C_ONES:C_ONES + P] = 1.0
    c[:, C_MIN:C_MIN + P] = np.where(j <= i, 3e38, 0.0)
    inv = (1.0 / np.float32(10000.0) ** (np.arange(0, D, 2, dtype=np.float32) / np.float32(D))).astype(np.float32)
    angle = (np.arange(N, dtype=np.float32)[:, None] * inv[None, :]).reshape(CH, P, D // 2).transpose(1, 0, 2)
    c[:, C_COS:C_SIN] = np.cos(angle).reshape(P, -1)
    c[:, C_SIN:C_NSIN] = np.sin(angle).reshape(P, -1)
    c[:, C_NSIN:C_RANK] = -np.sin(angle).reshape(P, -1)
    c[:, C_RANK:C_BASE] = E - np.arange(E)
    c[:, C_BASE:C_ALL] = CAP * np.arange(E)
    m = np.zeros((P, 2 * P), np.float32)
    m[:, 0:P] = j == i
    m[:, P:] = np.where(i <= j, 0.0, -BIG)
    return c, m


class Chain:

    def __init__(self, eng, sem, base):
        self.eng, self.sem, self.base, self.n = eng, sem, base, 0

    def __call__(self, ins):
        self.n += 1
        ins.then_inc(self.sem, 1)
        self.eng.wait_ge(self.sem, self.base + self.n)


def build(nc, x, wq, wkv, wo, wg, w1, w2, const, constb, out):
    ctx = ExitStack()
    with ctx:
        def sb(name, shape, dt=F32):
            return ctx.enter_context(nc.sbuf_tensor(name, shape, dt))

        def sem(name):
            return ctx.enter_context(nc.semaphore(name))

        xdisp = nc.dram_tensor("xdisp", [SLOTS, HID], F32).ap()
        ydisp = nc.dram_tensor("ydisp", [SLOTS, HID], F32).ap()

        acc = sb("acc", [P, TILES, HID])
        xn = sb("xn", [P, TILES, HID])
        xnT = sb("xnT", [P, KC, TOK])
        wq_sb = sb("wq_sb", [P, KV, KC, HD])
        wkv_sb = sb("wkv_sb", [P, KV, KC, 2 * D])
        wo_sb = sb("wo_sb", [P, KV, GROUPS, HID])
        wg_sb = sb("wg_sb", [P, KC, E])
        cst = sb("cst", [P, C_ALL])
        cstb = sb("cstb", [P, 2 * P], BF16)
        gate = sb("gate", [P, TOP_K, TILES])
        slot_in = sb("slot_in", [P, TOP_K, TILES], I32)
        slot_out = sb("slot_out", [P, TOP_K, TILES], I32)
        ARENA = 21900
        arena = sb("arena", [P, ARENA])
        at = [0]

        def take(n):
            at[0] += n
            assert at[0] <= ARENA, at[0]
            return arena[:, at[0] - n:at[0]]

        psS = ctx.enter_context(nc.psum_tensor("psS", [P, 2, 1024], F32))
        psR = ctx.enter_context(nc.psum_tensor("psR", [P, 3, 512], F32))
        psO = ctx.enter_context(nc.psum_tensor("psO", [P, 512], F32))
        psM = psR[:, 2, :]

        ident = cst[:, C_ID:C_ID + P]
        cum = cst[:, C_CUM:C_CUM + P]
        rank = cst[:, C_RANK:C_RANK + E].unsqueeze(1).broadcast_to([P, TILES, E])
        ebase = cst[:, C_BASE:C_BASE + E].unsqueeze(1).broadcast_to([P, TILES, E])
        identb, causalb = cstb[:, 0:P], cstb[:, P:2 * P]

        s_x = sem("s_x")
        s_cst = sem("s_cst")
        s_wg = sem("s_wg")
        s_wqkv = sem("s_wqkv")
        s_wo = sem("s_wo")

        at[0] = 0
        work = take(TILES * HID).rearrange("p (t d) -> p t d", t=TILES)
        zero = take(1024)
        stat = take(TILES * 8).rearrange("p (k t) -> p k t", k=8)
        small = [take(TILES * E).rearrange("p (t e) -> p t e", t=TILES) for _ in range(12)]
        tot_a = take(2 * TILES * E).rearrange("p (t e) -> p t e", e=E)
        tot_b = take(2 * TILES * E).rearrange("p (t e) -> p t e", e=E)
        rt = take(TILES * 12).rearrange("p (k t) -> p k t", k=12)

        s_zero = sem("s_zero")
        s_zfill = sem("s_zfill")
        s_a = sem("s_a")
        s_sq = sem("s_sq")
        s_std = sem("s_std")
        s_var = sem("s_var")
        s_cen = sem("s_cen")
        s_xn = sem("s_xn")
        s_tr = sem("s_tr")
        s_xnT = sem("s_xnT")
        s_lg = sem("s_lg")
        s_dl = sem("s_dl")
        s_pe = sem("s_pe")
        s_mask = sem("s_mask")
        s_pos = sem("s_pos")
        s_slots = sem("s_slots")
        s_scat = sem("s_scat")

        with nc.Block() as block:
            @block.sync
            def _(sp):
                sp.dma_start(acc[:, :, :], x.rearrange("(t p) d -> p t d", p=P)).then_inc(s_x, 16)
                sp.dma_start(cst[:, :], const).then_inc(s_cst, 16)
                sp.dma_start(cstb[:, :], constb).then_inc(s_cst, 16)
                sp.dma_start(wg_sb[:, :, :], wg).then_inc(s_wg, 16)
                sp.wait_ge(s_zero, 1)
                for e in range(SLOTS * HID // (P * 1024)):
                    rows = P * 1024 // HID
                    sp.dma_start(xdisp[e * rows:(e + 1) * rows, :].rearrange("(p r) d -> p (r d)", p=P),
                                 zero).then_inc(s_zfill, 16)
                sp.dma_start(wq_sb[:, :, :, :], wq).then_inc(s_wqkv, 16)
                sp.dma_start(wkv_sb[:, :, :, :], wkv).then_inc(s_wqkv, 16)
                sp.dma_start(wo_sb[:, :, :, :], wo).then_inc(s_wo, 16)

            @block.gpsimd
            def _(pool):
                pool.memset(zero, 0.0).then_inc(s_zero, 1)
                pool.wait_ge(s_slots, 1)
                pool.wait_ge(s_xn, 1)
                pool.wait_ge(s_zfill, 16 * (SLOTS * HID // (P * 1024)))
                for k in range(TOP_K):
                    for t in range(TILES):
                        pool.indirect_dma_start(
                            out=xdisp, out_offset=bass.IndirectOffsetOnAxis(ap=slot_in[:, k, t:t + 1], axis=0),
                            in_=xn[:, t, :], in_offset=None, bounds_check=SLOTS - 1,
                            oob_is_err=False).then_inc(s_scat, 16)
                pool.wait_ge(s_scat, 16 * TOP_K * TILES)

            @block.scalar
            def _(act):
                act.wait_ge(s_cen, 1)
                act.activation(xn[:, :, :], work, ACT.Square).then_inc(s_sq, 1)
                act.wait_ge(s_var, 1)
                act.activation(stat[:, 3, :], stat[:, 2, :], ACT.Sqrt).then_inc(s_std, 1)
                for i in range(TILES // 2):
                    act.wait_ge(s_tr, i + 1)
                    act.activation(xnT[:, :, 2 * i * P:2 * (i + 1) * P],
                                   psR[:, i % 2, :].rearrange("p (k t) -> p k t", k=KC), ACT.Copy).then_inc(s_xnT, 1)
                act.wait_ge(s_dl, 1)
                act.activation(small[1], small[0], ACT.Exp).then_inc(s_pe, 1)

            @block.tensor
            def _(pe):
                pe.wait_ge(s_cst, 32)
                pe.wait_ge(s_xn, 1)
                for i in range(TILES // 2):
                    if i >= 2:
                        pe.wait_ge(s_xnT, i - 1)
                    for k in range(KC):
                        for t in range(2):
                            last = pe.transpose(psR[:, i % 2, (k * 2 + t) * P:(k * 2 + t + 1) * P],
                                                xn[:, 2 * i + t, k * P:(k + 1) * P], ident)
                    last.then_inc(s_tr, 1)
                pe.wait_ge(s_xnT, TILES // 2)
                pe.wait_ge(s_wg, 16)
                for t in range(TILES):
                    for k in range(KC):
                        last = pe.matmul(psM[:, t * E:(t + 1) * E], xnT[:, k, t * P:(t + 1) * P], wg_sb[:, k, :],
                                         start=k == 0, stop=k == KC - 1)
                last.then_inc(s_lg, 1)
                pe.wait_ge(s_mask, 1)
                picked = small[5].rearrange("p t e -> p (t e)")
                pe.matmul(psM[:, 256:256 + TILES * E], cst[:, C_STRICT:C_STRICT + P], picked, start=True, stop=True)
                pe.matmul(psM[:, 384:384 + TILES * E], cst[:, C_ONES:C_ONES + P], picked, start=True, stop=True)\
                  .then_inc(s_pos, 1)

            @block.vector
            def _(dve):
                ch = Chain(dve, s_a, 0)

                def wide(v, n=HID):
                    return v.unsqueeze(2).broadcast_to([P, TILES, n])

                dve.wait_ge(s_x, 16)
                ch(dve.tensor_reduce(stat[:, 0, :], acc[:, :, :], AX.X, ALU.add))
                ch(dve.tensor_scalar(stat[:, 1, :], stat[:, 0, :], 1.0 / HID, None, ALU.mult))
                dve.tensor_tensor(work, acc[:, :, :], wide(stat[:, 1, :]), ALU.subtract).then_inc(s_cen, 1)
                dve.wait_ge(s_sq, 1)
                ch(dve.tensor_reduce(stat[:, 4, :], xn[:, :, :], AX.X, ALU.add))
                dve.tensor_scalar(stat[:, 2, :], stat[:, 4, :], 1.0 / HID, EPS, ALU.mult, ALU.add).then_inc(s_var, 1)
                dve.wait_ge(s_std, 1)
                ch(dve.reciprocal(stat[:, 5, :], stat[:, 3, :]))
                dve.tensor_tensor(xn[:, :, :], work, wide(stat[:, 5, :]), ALU.mult).then_inc(s_xn, 1)

                lg, lg2, eq, oh1, oh2, dl, pexp, slot, kept, tmp = (small[i] for i in (2, 3, 4, 6, 7, 0, 1, 8, 9, 10))
                m1, t1, m2, t2, den, r, e2 = (rt[:, i, :] for i in range(7))
                dve.wait_ge(s_lg, 1)
                ch(dve.tensor_copy(lg, psM[:, 0:TILES * E].rearrange("p (t e) -> p t e", e=E)))
                ch(dve.tensor_reduce(m1, lg, AX.X, ALU.max))
                dve.tensor_tensor(dl, lg, wide(m1, E), ALU.subtract).then_inc(s_dl, 1)
                ch(dve.tensor_tensor(eq, lg, wide(m1, E), ALU.is_equal))
                ch(dve.tensor_tensor(tmp, eq, rank, ALU.mult))
                ch(dve.tensor_reduce(t1, tmp, AX.X, ALU.max))
                ch(dve.tensor_tensor(oh1, tmp, wide(t1, E), ALU.is_equal))
                ch(dve.scalar_tensor_tensor(out=lg2, in0=oh1, scalar=-BIG, in1=lg, op0=ALU.mult, op1=ALU.add))
                ch(dve.tensor_reduce(m2, lg2, AX.X, ALU.max))
                ch(dve.tensor_tensor(eq, lg2, wide(m2, E), ALU.is_equal))
                ch(dve.tensor_tensor(tmp, eq, rank, ALU.mult))
                ch(dve.tensor_reduce(t2, tmp, AX.X, ALU.max))
                ch(dve.tensor_tensor(oh2, tmp, wide(t2, E), ALU.is_equal))
                dve.tensor_tensor(small[5], oh1, oh2, ALU.add).then_inc(s_mask, 1)
                dve.wait_ge(s_pe, 1)
                ch(dve.tensor_reduce(den, pexp, AX.X, ALU.add))
                ch(dve.reciprocal(r, den))
                ch(dve.tensor_tensor(tmp, pexp, oh2, ALU.mult))
                ch(dve.tensor_reduce(e2, tmp, AX.X, ALU.add))
                ch(dve.memset(tot_a, 0.0))
                ch(dve.memset(tot_b, 0.0))
                dve.wait_ge(s_pos, 1)
                ch(dve.tensor_copy(tot_a[:, TILES:, :], psM[:, 384:512].rearrange("p (t e) -> p t e", e=E)))
                src, dst, step = tot_a, tot_b, 1
                while step < TILES:
                    ch(dve.tensor_tensor(dst[:, TILES:, :], src[:, TILES:, :],
                                         src[:, TILES - step:2 * TILES - step, :], ALU.add))
                    src, dst, step = dst, src, 2 * step
                ch(dve.tensor_tensor(slot, psM[:, 256:384].rearrange("p (t e) -> p t e", e=E),
                                     src[:, TILES - 1:2 * TILES - 1, :], ALU.add))
                ch(dve.tensor_scalar(kept, slot, float(CAP), None, ALU.is_lt))
                ch(dve.tensor_tensor(slot, slot, ebase, ALU.add))
                prob = [r, e2]
                for k, oh in enumerate((oh1, oh2)):
                    s, kp, g = (rt[:, 7 + i, :] for i in range(3))
                    ch(dve.tensor_tensor(tmp, slot, oh, ALU.mult))
                    ch(dve.tensor_reduce(s, tmp, AX.X, ALU.add))
                    ch(dve.tensor_tensor(tmp, kept, oh, ALU.mult))
                    ch(dve.tensor_reduce(kp, tmp, AX.X, ALU.add))
                    ch(dve.tensor_tensor(slot_out[:, k, :], s, kp, ALU.mult))
                    ch(dve.scalar_tensor_tensor(out=g, in0=kp, scalar=-FAR, in1=s, op0=ALU.mult, op1=ALU.add))
                    ch(dve.tensor_scalar(slot_in[:, k, :], g, FAR, None, ALU.add))
                    if k:
                        ch(dve.tensor_tensor(kp, kp, e2, ALU.mult))
                    ch(dve.tensor_tensor(gate[:, k, :], kp, r, ALU.mult))
                dve.drain().then_inc(s_slots, 1)

        at[0] = 0
        w1_sb = take(2 * KC * FF).rearrange("p (s k f) -> p s k f", s=2, k=KC)
        w2_sb = take(2 * FC * HID).rearrange("p (s f d) -> p s f d", s=2, f=FC)
        xd = take(2 * ST * HID).rearrange("p (s t d) -> p s t d", s=2, t=ST)
        xdT = take(KC * CAP).rearrange("p (k n) -> p k n", k=KC)
        hT = take(FC * CAP).rearrange("p (f n) -> p f n", f=FC)
        yd = take(ST * HID).rearrange("p (t d) -> p t d", t=ST)

        s_w1 = [sem(f"s_w1_{s}") for s in range(2)]
        s_w2 = [sem(f"s_w2_{s}") for s in range(2)]
        s_xd = [sem(f"s_xd_{s}") for s in range(2)]
        s_xt = sem("s_xt")
        s_xdT = sem("s_xdT")
        s_h = sem("s_h")
        s_hT = sem("s_hT")
        s_y = sem("s_y")
        s_yd = sem("s_yd")
        s_ys = sem("s_ys")
        XT = 3
        YT = 3
        XD_DEPS = 1

        xd_v = xdisp.rearrange("(e t p) d -> e p t d", e=E, p=P)
        yd_v = ydisp.rearrange("(e t p) d -> e p t d", e=E, p=P)

        with nc.Block() as block:
            @block.sync
            def _(sp):
                for s in range(2):
                    sp.dma_start(xd[:, s, :, :], xd_v[s]).then_inc(s_xd[s], 16)
                    sp.dma_start(w1_sb[:, s, :, :], w1[s]).then_inc(s_w1[s], 16)
                    sp.dma_start(w2_sb[:, s, :, :], w2[s]).then_inc(s_w2[s], 16)
                with sp.Fori(1, E // 2) as i:
                    for s in range(2):
                        e = 2 * i + s
                        sp.wait_ge(s_y, (e - 1) * YT)
                        sp.dma_start(xd[:, s, :, :], xd_v[bass.ds(e, 1)]).then_inc(s_xd[s], 16)
                        sp.dma_start(w1_sb[:, s, :, :], w1[bass.ds(e, 1)]).then_inc(s_w1[s], 16)
                        sp.dma_start(w2_sb[:, s, :, :], w2[bass.ds(e, 1)]).then_inc(s_w2[s], 16)

            @block.tensor
            def _(pe):
                with pe.Fori(0, E // 2) as i:
                    for s in range(2):
                        e = 2 * i + s
                        pe.wait_ge(s_xd[s], 16 * i + 16)
                        for j in range(XT):
                            pe.wait_ge(s_xdT, START + e * XT + max(j - 1, 0))
                            for t in range(2 * j, min(2 * j + 2, ST)):
                                for k in range(KC):
                                    last = pe.transpose(psR[:, j % 2, ((t % 2) * KC + k) * P:((t % 2) * KC + k + 1) * P],
                                                        xd[:, s, t, k * P:(k + 1) * P], ident)
                            last.then_inc(s_xt, 1)
                        pe.wait_ge(s_xdT, START + (e + 1) * XT)
                        pe.wait_ge(s_w1[s], 16 * i + 16)
                        for f in range(FC):
                            pe.wait_ge(s_hT, START + e * FC + max(f - 1, 0))
                            for n in range(2):
                                for k in range(KC):
                                    last = pe.matmul(psS[:, f % 2, n * 512:n * 512 + HALF],
                                                     w1_sb[:, s, k, f * P:(f + 1) * P],
                                                     xdT[:, k, n * HALF:(n + 1) * HALF],
                                                     start=k == 0, stop=k == KC - 1)
                            last.then_inc(s_h, 1)
                        pe.wait_ge(s_hT, START + (e + 1) * FC)
                        pe.wait_ge(s_w2[s], 16 * i + 16)
                        for j in range(YT):
                            pe.wait_ge(s_yd, START + e * YT + max(j - 1, 0))
                            bank = (psM, psO)[j % 2]
                            for t in range(2 * j, min(2 * j + 2, ST)):
                                for f in range(FC):
                                    last = pe.matmul(bank[:, (t % 2) * HID:(t % 2 + 1) * HID],
                                                     hT[:, f, t * P:(t + 1) * P], w2_sb[:, s, f, :],
                                                     start=f == 0, stop=f == FC - 1)
                            last.then_inc(s_y, 1)

            @block.vector
            def _(dve):
                dve.sem_inc(s_xdT, START)
                dve.sem_inc(s_hT, START)
                with dve.Fori(0, E // 2) as i:
                    for s in range(2):
                        e = 2 * i + s
                        for j in range(XT):
                            nt = min(2, ST - 2 * j)
                            dve.wait_ge(s_xt, e * XT + j + 1)
                            dve.tensor_copy(
                                xdT[:, :, 2 * j * P:(2 * j + nt) * P].rearrange("p k (t n) -> p t k n", n=P),
                                psR[:, j % 2, 0:nt * KC * P].rearrange("p (t k n) -> p t k n", k=KC, n=P))\
                               .then_inc(s_xdT, 1)
                        for f in range(FC):
                            dve.wait_ge(s_h, e * FC + f + 1)
                            dve.tensor_scalar(hT[:, f, :].rearrange("p (n c) -> p n c", n=2),
                                              psS[:, f % 2, :].rearrange("p (n c) -> p n c", n=2)[:, :, 0:HALF],
                                              0.0, None, ALU.max).then_inc(s_hT, 1)

            @block.scalar
            def _(act):
                act.sem_inc(s_yd, START)
                act.sem_inc(s_ys, START)
                with act.Fori(0, E // 2) as i:
                    for s in range(2):
                        e = 2 * i + s
                        act.wait_ge(s_ys, START + 16 * e)
                        for j in range(YT):
                            nt = min(2, ST - 2 * j)
                            act.wait_ge(s_y, e * YT + j + 1)
                            act.activation(yd[:, 2 * j:2 * j + nt, :],
                                           (psM, psO[:, :])[j % 2][:, 0:nt * HID].rearrange("p (t d) -> p t d", t=nt),
                                           ACT.Copy).then_inc(s_yd, 1)
                        act.wait_ge(s_yd, START + (e + 1) * YT)
                        act.dma_start(yd_v[bass.ds(e, 1)], yd).then_inc(s_ys, 16)
                act.wait_ge(s_ys, START + 16 * E)

        at[0] = 0
        xst = take(2 * KC * P).rearrange("p (s k t) -> p s k t", s=2, k=KC)
        qk_sb = take((GROUPS + 1) * D).rearrange("p (h d) -> p h d", d=D)
        qk_exp = take((GROUPS + 1) * D).rearrange("p (h d) -> p h d", d=D)
        qk_soft = take((GROUPS + 1) * D).rearrange("p (h d) -> p h d", d=D)
        rope_a = take((GROUPS + 1) * D).rearrange("p (h d) -> p h d", d=D)
        rope_b = take((GROUPS + 1) * D).rearrange("p (h d) -> p h d", d=D)
        qk_rot = take((GROUPS + 1) * D).rearrange("p (h d) -> p h d", d=D)
        nmx = take(8)
        den = take(8)
        rden = take(8)
        kabs = take(D)
        kex = take(D)
        kln = take(D)
        klog = take(D)
        dec_p = take(P)
        dec_n = take(P)
        edge = take(2 * 8).rearrange("p (s k) -> p s k", s=2)
        qT = take(2 * HD).rearrange("p (s n) -> p s n", s=2)
        kT = take(N)
        kT_first = take(P)
        v_sb = take(CH * D).rearrange("p (c d) -> p c d", d=D)
        v_first = take(2 * D).rearrange("p (c d) -> p c d", d=D)
        qdT = take(2 * HD).rearrange("p (s n) -> p s n", s=2)
        kdT = take(P)
        kd = take(P)
        am = take(2 * HD).rearrange("p (s n) -> p s n", s=2)
        state = take(2 * D).rearrange("p (s n) -> p s n", s=2)
        state_sum = take(D)
        state_raw = take(D)
        prob = take(2 * N).rearrange("p (s n) -> p s n", s=2)
        hmx = take(GROUPS * 2)
        hden = take(GROUPS * 2)
        hrec = take(GROUPS * 2)
        pT = take(2 * CH * 2 * P).rearrange("p (s c h q) -> p s c h q", s=2, c=CH, h=2)
        oT = take(HD)
        GT = TILES // (B * KV)
        rows = take(TOP_K * GT * HID).rearrange("p (k t d) -> p k t d", k=TOP_K, t=GT)
        row_slot = sb("row_slot", [P, TOP_K, GT], I32)
        row_gate = take(TOP_K * GT).rearrange("p (k t) -> p k t", k=TOP_K)
        cos = cst[:, C_COS:C_SIN].rearrange("p (c d) -> p c d", c=CH)
        sin = cst[:, C_SIN:C_NSIN].rearrange("p (c d) -> p c d", c=CH)
        nsin = cst[:, C_NSIN:C_RANK].rearrange("p (c d) -> p c d", c=CH)

        xst_ready = sem("xst_ready")
        max_ready = sem("max_ready")
        k_copied = sem("k_copied")
        q_copied = sem("q_copied")
        v_ready = sem("v_ready")
        kln_ready = sem("kln_ready")
        den_ready = sem("den_ready")
        klog_ready = sem("klog_ready")
        rden_ready = sem("rden_ready")
        soft_ready = sem("soft_ready")
        rot_ready = sem("rot_ready")
        rfill = sem("rfill")
        dec_ready = sem("dec_ready")
        qT_ready = sem("qT_ready")
        kT_ready = sem("kT_ready")
        qdT_ready = sem("qdT_ready")
        kdT_ready = sem("kdT_ready")
        kd_ready = sem("kd_ready")
        am_ready = sem("am_ready")
        raw_ready = sem("raw_ready")
        state_ready = sem("state_ready")
        first_moved = sem("first_moved")
        scored = sem("scored")
        hmax_ready = sem("hmax_ready")
        exped = sem("exped")
        hrec_ready = sem("hrec_ready")
        scaled = sem("scaled")
        pT_act = sem("pT_act")
        pT_dve = sem("pT_dve")
        pv_done = sem("pv_done")
        oT_ready = sem("oT_ready")
        acc_done = sem("acc_done")
        slot_ready = sem("slot_ready")
        rows_asked = sem("rows_asked")
        gathered = sem("gathered")
        row_gate_ready = sem("row_gate_ready")
        rows_added = sem("rows_added")
        act_own = sem("act_own")
        pool_own = sem("pool_own")
        dve_own = sem("dve_own")

        def turn_list(p):
            return [(what, p) for what in ("cum", "qrot", "krot", "qsoft", "ksoft")]

        def linear_list(p):
            return [("att", p)] + [("kd", p), ("outer", p)] * (p % CH < CH - 1)

        BANKS = 3
        before = [("q", 0), ("kv", 0)] + turn_list(0) + linear_list(0) + [("q", 1), ("kv", 1)]
        turns = []

        def probs_list(c, h):
            return [("pa", (c - 4) * GROUPS + h)] * (c >= 4) + [("pd", c * GROUPS + h)]

        for c in range(CH):
            turns += [("cum", c + 1)] + probs_list(c, 0)
            turns += [("qrot", c + 1), ("krot", c + 1), ("qsoft", c + 1), ("ksoft", c + 1)]
            turns += [("out", c - 1)] * (c > 0) + probs_list(c, 1)
            rest = linear_list(c + 1)
            turns += rest[:2] + [("q", c + 2), ("kv", c + 2)] + probs_list(c, 2)
            turns += rest[2:] + probs_list(c, 3)
        turns.append(("out", CH - 1))
        R0, RT = len(before), len(turns)
        turns += [None] * (-RT % BANKS)
        READ_BY = {"q": (q_copied, CH), "kv": (v_ready, CH), "cum": (dec_ready, CH), "qrot": (qT_ready, CH),
                   "krot": (kT_ready, CH), "qsoft": (qdT_ready, CH), "ksoft": (kdT_ready, CH), "att": (am_ready, CH),
                   "kd": (kd_ready, CH - 1), "outer": (raw_ready, CH - 1), "pa": (pT_act, 4 * GROUPS),
                   "pd": (pT_dve, CH * GROUPS), "out": (acc_done, CH)}

        def nth(p):
            return p - p // CH

        def place(key):
            return R0 + turns.index(key) if key in turns else before.index(key)

        def bank(*key):
            return psR[:, (place(key) - R0) % BANKS, :]

        def filled(eng, g, *key):
            eng.wait_ge(rfill, START + g * RT + place(key) + 1)

        def keys_of(c):
            return kT_first if c % CH == 0 else kT

        def values_of(p):
            return v_first[:, p % CH, :] if p % CH < 2 else v_sb[:, p % CH, :]

        with nc.Block() as block:
            @block.tensor
            def _(pe):
                def begin(g, *key):
                    n = place(key) - R0
                    if n < 0:
                        last = [(before[n + R0 - BANKS], 0)] if n + R0 >= BANKS else []
                    elif n >= BANKS:
                        last = [(turns[n - BANKS], 0)]
                    else:
                        m = len(turns) + n - BANKS
                        last = [(before[n + R0 - BANKS], 0), (turns[m] or turns[m - BANKS], 1)]
                    for (what, i), groups_ago in last:
                        read, times = READ_BY[what]
                        count = (nth(i) if what in ("kd", "outer") else i) + 1 - groups_ago * times
                        pe.wait_ge(read, START + g * times + max(count, 0))
                    return bank(*key)

                def project(g, p):
                    head = (g + p // CH) & (KV - 1)
                    pe.wait_ge(xst_ready, START + g * CH + p + 1)
                    r = begin(g, "q", p)
                    for k in range(KC):
                        last = pe.matmul(r, xst[:, p % 2, k, :], wq_sb[:, bass.ds(head, 1), k, :],
                                         start=k == 0, stop=k == KC - 1)
                    last.then_inc(rfill, 1)
                    r = begin(g, "kv", p)
                    for k in range(KC):
                        last = pe.matmul(r[:, 0:2 * D], xst[:, p % 2, k, :], wkv_sb[:, bass.ds(head, 1), k, :],
                                         start=k == 0, stop=k == KC - 1)
                    last.then_inc(rfill, 1)

                def sum_decays(g, p):
                    u = g * CH + p
                    pe.wait_ge(klog_ready, START + u + 1)
                    r = begin(g, "cum", p)
                    pe.matmul(r[:, 0:P], klog, cum, start=True, stop=True).then_inc(rfill, 1)

                def turn_rotated(g, p):
                    u = g * CH + p
                    pe.wait_ge(rot_ready, START + u + 1)
                    r = begin(g, "qrot", p)
                    for h in range(GROUPS):
                        last = pe.transpose(r[:, h * P:(h + 1) * P], qk_rot[:, h, :], ident)
                    last.then_inc(rfill, 1)
                    r = begin(g, "krot", p)
                    pe.transpose(r[:, 0:P], qk_rot[:, GROUPS, :], ident).then_inc(rfill, 1)

                def turn_soft(g, p):
                    u = g * CH + p
                    pe.wait_ge(soft_ready, START + u + 1)
                    r = begin(g, "qsoft", p)
                    for h in range(GROUPS):
                        last = pe.transpose(r[:, h * P:(h + 1) * P], qk_soft[:, h, :], ident)
                    last.then_inc(rfill, 1)
                    r = begin(g, "ksoft", p)
                    pe.transpose(r[:, 0:P], qk_soft[:, GROUPS, :], ident).then_inc(rfill, 1)

                def linear(g, p):
                    u = g * CH + p
                    pe.wait_ge(kdT_ready, START + u + 1)
                    pe.wait_ge(qdT_ready, START + u + 1)
                    pe.wait_ge(v_ready, START + u + 1)
                    r = begin(g, "att", p)
                    pe.matmul(r, kdT, qdT[:, p % 2, :], start=True, stop=True).then_inc(rfill, 1)
                    if p % CH < CH - 1:
                        r = begin(g, "kd", p)
                        pe.transpose(r[:, 0:P], kdT, ident).then_inc(rfill, 1)

                def outer(g, p):
                    if p % CH < CH - 1:
                        u = g * CH + p
                        pe.wait_ge(kd_ready, START + g * (CH - 1) + nth(p) + 1)
                        r = begin(g, "outer", p)
                        pe.matmul(r[:, 0:D], kd, values_of(p), start=True, stop=True).then_inc(rfill, 1)

                def score(g, c, h):
                    n = c * GROUPS + h
                    if h == 0:
                        pe.wait_ge(qT_ready, START + g * CH + c + 1)
                        pe.wait_ge(kT_ready, START + g * CH + c + 1)
                        if c == 1:
                            pe.wait_ge(first_moved, START + 2 * g + 2)
                    if n >= 2:
                        pe.wait_ge(exped, START + g * CH * GROUPS + n - 1)
                    keys = (c % CH + 1) * P
                    q, k = qT[:, c % 2, h * P:(h + 1) * P], keys_of(c)
                    for k0 in range(0, keys - P, 512):
                        k1 = min(k0 + 512, keys - P)
                        pe.matmul(psS[:, h % 2, k0:k1], q, k[:, k0:k1], start=True, stop=True)
                    own = psS[:, h % 2, keys - P:keys]
                    pe.matmul(own, q, k[:, keys - P:keys], start=True, stop=False)
                    pe.matmul(own, identb, causalb, start=False, stop=True).then_inc(scored, 1)

                def turn_probs(g, c, h):
                    n = c * GROUPS + h
                    pe.wait_ge(scaled, START + g * CH * GROUPS + n + 1)
                    k0 = 0
                    if c >= 4:
                        r = begin(g, "pa", n - 4 * GROUPS)
                        for kb in range(4):
                            last = pe.transpose(r[:, kb * P:(kb + 1) * P], prob[:, h % 2, kb * P:(kb + 1) * P], ident)
                        last.then_inc(rfill, 1)
                        k0 = 4
                    r = begin(g, "pd", n)
                    for kb in range(k0, c + 1):
                        last = pe.transpose(r[:, (kb - k0) * P:(kb - k0 + 1) * P],
                                            prob[:, h % 2, kb * P:(kb + 1) * P], ident)
                    last.then_inc(rfill, 1)

                def weigh(g, c, j):
                    u = g * CH + c
                    cols = slice(j * 2 * P, (j + 1) * 2 * P)
                    if j == 0:
                        pe.wait_ge(oT_ready, START + u)
                    if c:
                        pe.wait_ge(state_ready, START + g * (CH - 1) + c)
                        pe.matmul(psO[:, cols], state[:, c % 2, :], qdT[:, c % 2, cols], start=True, stop=False)
                    if c >= 4:
                        pe.wait_ge(pT_act, START + g * 4 * GROUPS + (c - 4) * GROUPS + 2 * j + 2)
                    pe.wait_ge(pT_dve, START + u * GROUPS + 2 * j + 2)
                    for kb in range(c + 1):
                        last = pe.matmul(psO[:, cols], values_of(0) if c == 0 else v_sb[:, kb, :],
                                         pT[:, j, kb, :, :].rearrange("p h q -> p (h q)"),
                                         start=c == 0, stop=kb == c)
                    last.then_inc(pv_done, 1)

                def outputs(g, c):
                    pe.wait_ge(oT_ready, START + g * CH + c + 1)
                    r = begin(g, "out", c)
                    for h in range(GROUPS):
                        last = pe.matmul(r[:, 0:HID], oT[:, h * P:(h + 1) * P],
                                         wo_sb[:, bass.ds(g & (KV - 1), 1), h, :],
                                         start=h == 0, stop=h == GROUPS - 1)
                    last.then_inc(rfill, 1)

                pe.wait_ge(s_wqkv, 32)
                pe.wait_ge(s_wo, 16)
                for counted in (rfill, scored, pv_done):
                    pe.sem_inc(counted, START)
                project(0, 0)
                sum_decays(0, 0)
                turn_rotated(0, 0)
                turn_soft(0, 0)
                linear(0, 0)
                outer(0, 0)
                project(0, 1)
                score(0, 0, 0)
                score(0, 0, 1)
                with pe.Fori(0, B * KV) as g:
                    for c in range(CH):
                        sum_decays(g, c + 1)
                        if c:
                            score(g, c, 1)
                            weigh(g, c - 1, 1)
                        turn_probs(g, c, 0)
                        turn_rotated(g, c + 1)
                        score(g, c, 2)
                        turn_soft(g, c + 1)
                        if c:
                            outputs(g, c - 1)
                        turn_probs(g, c, 1)
                        linear(g, c + 1)
                        score(g, c, 3)
                        weigh(g, c, 0)
                        project(g, c + 2)
                        turn_probs(g, c, 2)
                        outer(g, c + 1)
                        score(g, c + 1, 0)
                        turn_probs(g, c, 3)
                    score(g, CH, 1)
                    weigh(g, CH - 1, 1)
                    outputs(g, CH - 1)

            @block.scalar
            def _(act):
                def read_qkv(g, p):
                    filled(act, g, "q", p)
                    act.wait_ge(rot_ready, START + g * CH + p)
                    act.wait_ge(klog_ready, START + g * CH + p)
                    act.wait_ge(max_ready, START + g * CH + p)
                    act.activation(qk_sb[:, 0:GROUPS, :].rearrange("p h d -> p (h d)"), bank("q", p), ACT.Copy)                       .then_inc(q_copied, 1)
                    filled(act, g, "kv", p)
                    act.activation(qk_sb[:, GROUPS, :], bank("kv", p)[:, 0:D], ACT.Copy).then_inc(k_copied, 1)
                    if p < CH:
                        act.wait_ge(pv_done, START + g * 2 * CH)
                    else:
                        act.wait_ge(first_moved, START + 2 * g + 2)
                    act.activation(values_of(p), bank("kv", p)[:, D:2 * D], ACT.Copy).then_inc(v_ready, 1)

                def soften(g, p, heads):
                    u = g * CH + p
                    act.wait_ge(soft_ready, START + u)
                    act.wait_ge(max_ready, START + u + 1)
                    for h in heads:
                        last = act.activation(qk_exp[:, h, :], qk_sb[:, h, :], ACT.Exp,
                                              bias=nmx[:, h:h + 1], accum_out=den[:, h:h + 1])
                    last.then_inc(den_ready, 1)

                def log_sigmoid(own, g, p):
                    act.wait_ge(k_copied, START + g * CH + p + 1)
                    own(act.activation(kabs, qk_sb[:, GROUPS, :], ACT.Abs))
                    own(act.activation(kex, kabs, ACT.Exp, scale=-1.0))
                    act.activation(kln, kex, ACT.Ln, bias=1.0).then_inc(kln_ready, 1)

                def decays(own, g, p):
                    u = g * CH + p
                    filled(act, g, "cum", p)
                    G, e = bank("cum", p), edge[:, p % 2, :]
                    act.wait_ge(raw_ready, START + g * (CH - 1) + max(nth(p) - 1, 0))
                    if p > 1:
                        act.wait_ge(state_ready, START + g * (CH - 1) + p - 2)
                    act.activation(e[:, 0:1], G[:, MID:MID + 1], ACT.Copy)
                    own(act.activation(e[:, 1:2], G[:, MID:MID + 1], ACT.Copy, scale=-1.0))
                    act.activation(e[:, 2:3], G[:, MID:MID + 1], ACT.Exp)
                    act.activation(e[:, 3:4], G[:, P - 1:P], ACT.Exp, bias=e[:, 1:2])
                    act.wait_ge(qdT_ready, START + u)
                    act.wait_ge(kdT_ready, START + u)
                    act.activation(dec_n, G[:, 0:P], ACT.Exp, scale=-1.0, bias=e[:, 0:1])
                    act.activation(dec_p, G[:, 0:P], ACT.Exp, bias=e[:, 1:2]).then_inc(dec_ready, 1)

                def rotated(g, p):
                    filled(act, g, "qrot", p)
                    act.wait_ge(scored, START + GROUPS * (g * CH + max(p - 1, 0)))
                    act.activation(qT[:, p % 2, :], bank("qrot", p), ACT.Copy, scale=SCALE).then_inc(qT_ready, 1)
                    filled(act, g, "krot", p)
                    if p == CH:
                        act.wait_ge(first_moved, START + 2 * g + 2)
                    dst = kT_first if p % CH == 0 else kT[:, p * P:(p + 1) * P]
                    act.activation(dst, bank("krot", p)[:, 0:P], ACT.Copy).then_inc(kT_ready, 1)

                def exps(g, c, h):
                    n = c * GROUPS + h
                    keys = (c % CH + 1) * P
                    act.wait_ge(hmax_ready, START + g * CH * GROUPS + n + 1)
                    if n >= 2:
                        filled(act, g, "pd", n - 2)
                    i = (c % 2) * GROUPS + h
                    act.activation(prob[:, h % 2, 0:keys], psS[:, h % 2, 0:keys], ACT.Exp, bias=hmx[:, i:i + 1],
                                   accum_out=hden[:, i:i + 1]).then_inc(exped, 1)

                def columns(g, c, h):
                    if c >= 4:
                        n = (c - 4) * GROUPS + h
                        filled(act, g, "pa", n)
                        act.wait_ge(pv_done, START + 2 * (g * CH + c - 1) + h // 2 + 1)
                        act.activation(pT[:, h // 2, 0:4, h % 2, :], bank("pa", n).rearrange("p (k q) -> p k q", k=4),
                                       ACT.Copy).then_inc(pT_act, 1)

                def turned_keys(g, p):
                    if p % CH < CH - 1:
                        filled(act, g, "kd", p)
                        act.activation(kd, bank("kd", p)[:, 0:P], ACT.Copy).then_inc(kd_ready, 1)

                def read_out(g, c):
                    act.wait_ge(pv_done, START + 2 * (g * CH + c + 1))
                    act.activation(oT, psO[:, :], ACT.Copy).then_inc(oT_ready, 1)

                for counted in (k_copied, q_copied, v_ready, kln_ready, den_ready, dec_ready, qT_ready,
                                kT_ready, kd_ready, exped, pT_act, oT_ready, act_own):
                    act.sem_inc(counted, START)
                act.add_instruction(mybir.InstLoadActFuncSet(name=nc.get_next_instruction_name(),
                                                             engine=mybir.EngineType.Activation,
                                                             act_func_set_id=EXP_AND_LN))
                own = Chain(act, act_own, START)
                for p in range(2):
                    read_qkv(0, p)
                    log_sigmoid(own, 0, p)
                    soften(0, p, range(0, 3))
                    soften(0, p, range(3, GROUPS + 1))
                    if p == 0:
                        decays(own, 0, p)
                        rotated(0, p)
                        turned_keys(0, p)
                exps(0, 0, 0)
                exps(0, 0, 1)
                first = own.n
                with act.Fori(0, B * KV) as g:
                    own = Chain(act, act_own, START + first + g * 3 * CH)
                    for c in range(CH):
                        decays(own, g, c + 1)
                        if c:
                            exps(g, c, 1)
                            read_out(g, c - 1)
                        columns(g, c, 0)
                        rotated(g, c + 1)
                        exps(g, c, 2)
                        columns(g, c, 1)
                        turned_keys(g, c + 1)
                        exps(g, c, 3)
                        read_qkv(g, c + 2)
                        log_sigmoid(own, g, c + 2)
                        columns(g, c, 2)
                        soften(g, c + 2, range(0, 3))
                        exps(g, c + 1, 0)
                        columns(g, c, 3)
                        soften(g, c + 2, range(3, GROUPS + 1))
                    exps(g, CH, 1)
                    read_out(g, CH - 1)
                    assert own.n == 3 * CH

            @block.vector
            def _(dve):
                causal_min = cst[:, C_MIN:C_MIN + P].unsqueeze(1).broadcast_to([P, GROUPS, P])

                def channel_max(g, p):
                    dve.wait_ge(k_copied, START + g * CH + p + 1)
                    dve.wait_ge(den_ready, START + 2 * (g * CH + p))
                    dve.tensor_reduce(nmx[:, 0:GROUPS + 1], qk_sb, AX.X, ALU.max, negate=True).then_inc(max_ready, 1)

                def log_decay(g, p):
                    dve.wait_ge(kln_ready, START + g * CH + p + 1)
                    if p:
                        filled(dve, g, "cum", p - 1)
                    dve.scalar_tensor_tensor(out=klog, in0=qk_sb[:, GROUPS, :], scalar=0.0, in1=kln, op0=ALU.min,
                                             op1=ALU.subtract).then_inc(klog_ready, 1)

                def soft_sums(g, p):
                    dve.wait_ge(den_ready, START + 2 * (g * CH + p + 1))
                    dve.wait_ge(soft_ready, START + g * CH + p)
                    dve.reciprocal(rden[:, 0:GROUPS + 1], den[:, 0:GROUPS + 1]).then_inc(rden_ready, 1)

                def start_state(g, p):
                    if p % CH:
                        dve.wait_ge(dec_ready, START + g * CH + p + 1)
                        dve.wait_ge(raw_ready, START + g * (CH - 1) + p)
                        dve.wait_ge(pv_done, START + 2 * (g * CH + p - 1))
                        dve.tensor_scalar(state[:, p % 2, :], state_raw, edge[:, p % 2, 2:3], None, ALU.mult)\
                           .then_inc(state_ready, 1)

                def decayed(g, p):
                    u = g * CH + p
                    dve.wait_ge(dec_ready, START + u + 1)
                    filled(dve, g, "qsoft", p)
                    dve.wait_ge(pv_done, START + 2 * (g * CH + max(p - 1, 0)))
                    dve.tensor_tensor(qdT[:, p % 2, :].rearrange("p (h t) -> p h t", t=P),
                                      bank("qsoft", p).rearrange("p (h t) -> p h t", t=P),
                                      dec_p.unsqueeze(1).broadcast_to([P, GROUPS, P]), ALU.mult).then_inc(qdT_ready, 1)
                    filled(dve, g, "ksoft", p)
                    dve.tensor_tensor(kdT, bank("ksoft", p)[:, 0:P], dec_n, ALU.mult).then_inc(kdT_ready, 1)

                def masked(g, p):
                    filled(dve, g, "att", p)
                    dve.tensor_tensor(am[:, p % 2, :].rearrange("p (h t) -> p h t", t=P),
                                      bank("att", p).rearrange("p (h t) -> p h t", t=P), causal_min,
                                      ALU.min).then_inc(am_ready, 1)

                def add_state(own, g, p):
                    if p % CH < CH - 1:
                        filled(dve, g, "outer", p)
                        m = bank("outer", p)[:, 0:D]
                        if p % CH:
                            own(dve.tensor_tensor(state_sum, m, state[:, p % 2, :], ALU.add))
                            m = state_sum
                        dve.tensor_scalar(state_raw, m, edge[:, p % 2, 3:4], None, ALU.mult).then_inc(raw_ready, 1)

                def head_max(g, c, h):
                    dve.wait_ge(scored, START + (g * CH + c) * GROUPS + h + 1)
                    i = (c % 2) * GROUPS + h
                    dve.tensor_reduce(hmx[:, i:i + 1], psS[:, h % 2, 0:(c % CH + 1) * P], AX.X, ALU.max, negate=True)\
                       .then_inc(hmax_ready, 1)

                def head_sum(g, c, h):
                    n = START + (g * CH + c) * GROUPS + h + 1
                    dve.wait_ge(exped, n)
                    i = (c % 2) * GROUPS + h
                    dve.reciprocal(hrec[:, i:i + 1], hden[:, i:i + 1]).then_inc(hrec_ready, 1)
                    dve.wait_ge(hrec_ready, n)
                    pr = prob[:, h % 2, 0:(c + 1) * P]
                    dve.tensor_scalar(pr, pr, hrec[:, i:i + 1], None, ALU.mult).then_inc(scaled, 1)

                def columns(g, c, h):
                    n = c * GROUPS + h
                    filled(dve, g, "pd", n)
                    dve.wait_ge(pv_done, START + (2 * (g * CH + c - 1) + h // 2 + 1 if c else 2 * CH * g))
                    r, k0 = bank("pd", n), 4 if c >= 4 else 0
                    if c > k0:
                        dve.tensor_copy(pT[:, h // 2, k0:c, h % 2, :], r[:, 0:(c - k0) * P].rearrange("p (k q) -> p k q", q=P))
                    dve.wait_ge(am_ready, START + g * CH + c + 1)
                    dve.tensor_tensor(pT[:, h // 2, c, h % 2, :], r[:, (c - k0) * P:(c - k0 + 1) * P],
                                      am[:, c % 2, h * P:(h + 1) * P], ALU.add).then_inc(pT_dve, 1)

                def add_out(g, c):
                    filled(dve, g, "out", c)
                    dve.wait_ge(rows_added, START + TOP_K * GT * g)
                    dve.wait_ge(acc_done, START + g * CH)
                    rows_c = acc[:, bass.ds(((g >> 2) & (B - 1)) * CH + c, 1), :].rearrange("p t d -> p (t d)")
                    dve.scalar_tensor_tensor(out=rows_c, in0=bank("out", c)[:, 0:HID], scalar=0.5, in1=rows_c,
                                             op0=ALU.mult, op1=ALU.add).then_inc(acc_done, 1)

                def add_rows(g):
                    dve.tensor_copy(row_gate, gate[:, :, bass.ds(g * GT, GT)]).then_inc(row_gate_ready, 1)
                    dve.wait_ge(row_gate_ready, START + g + 1)
                    dve.wait_ge(gathered, 16 * TOP_K * GT * (g + 1))
                    dve.wait_ge(acc_done, START + g * CH + CH)
                    for k in range(TOP_K):
                        for t in range(GT):
                            if k:
                                dve.wait_ge(rows_added, START + TOP_K * GT * g + GT * (k - 1) + t + 1)
                            rows_t = acc[:, bass.ds(g * GT + t, 1), :].rearrange("p t d -> p (t d)")
                            dve.scalar_tensor_tensor(out=rows_t, in0=rows[:, k, t, :], scalar=row_gate[:, k, t:t + 1],
                                                     in1=rows_t, op0=ALU.mult, op1=ALU.add).then_inc(rows_added, 1)

                def move_first(g):
                    dve.wait_ge(pv_done, START + g * 2 * CH)
                    dve.wait_ge(v_ready, START + g * CH + 2)
                    dve.tensor_copy(v_sb[:, 0:2, :], v_first).then_inc(first_moved, 1)
                    dve.wait_ge(kT_ready, START + g * CH + 1)
                    dve.tensor_copy(kT[:, 0:P], kT_first).then_inc(first_moved, 1)

                for counted in (max_ready, first_moved, klog_ready, rden_ready, qdT_ready, kdT_ready, am_ready,
                                raw_ready, state_ready, hmax_ready, hrec_ready, scaled, pT_dve, acc_done,
                                row_gate_ready, rows_added, dve_own):
                    dve.sem_inc(counted, START)
                own = Chain(dve, dve_own, START)
                for p in range(2):
                    channel_max(0, p)
                    log_decay(0, p)
                    soft_sums(0, p)
                    if p == 0:
                        decayed(0, p)
                        masked(0, p)
                        add_state(own, 0, p)
                head_max(0, 0, 0)
                head_max(0, 0, 1)
                assert own.n == 0
                with dve.Fori(0, B * KV) as g:
                    own = Chain(dve, dve_own, START + g * (CH - 2))
                    for c in range(CH):
                        head_sum(g, c, 0)
                        if c:
                            head_max(g, c, 1)
                        columns(g, c, 0)
                        if c == 0:
                            move_first(g)
                        head_sum(g, c, 1)
                        head_max(g, c, 2)
                        start_state(g, c + 1)
                        decayed(g, c + 1)
                        if c:
                            add_out(g, c - 1)
                        columns(g, c, 1)
                        masked(g, c + 1)
                        head_sum(g, c, 2)
                        head_max(g, c, 3)
                        channel_max(g, c + 2)
                        columns(g, c, 2)
                        log_decay(g, c + 2)
                        head_sum(g, c, 3)
                        add_state(own, g, c + 1)
                        head_max(g, c + 1, 0)
                        columns(g, c, 3)
                        soft_sums(g, c + 2)
                    head_max(g, CH, 1)
                    add_out(g, CH - 1)
                    add_rows(g)
                    assert own.n == CH - 2

            @block.gpsimd
            def _(pool):
                half = D // 2

                def stage(g, p):
                    b = ((g + p // CH) >> 2) & (B - 1)
                    if p >= 2:
                        filled(pool, g, "kv", p - 2) if p - 2 >= 2 else pool.wait_ge(v_ready, START + g * CH + p - 1)
                    pool.tensor_copy(xst[:, p % 2, :, :], xnT[:, :, bass.ds(b * N + (p % CH) * P, P)])\
                        .then_inc(xst_ready, 1)

                def rotate(own, g, p):
                    u = g * CH + p

                    def table(t, n):
                        return t[:, p % CH, :].unsqueeze(1).broadcast_to([P, n, half])

                    pool.wait_ge(k_copied, START + u + 1)
                    pool.wait_ge(q_copied, START + u + 1)
                    pool.tensor_tensor(rope_a.rearrange("p h (i d) -> p (h i) d", i=2),
                                       qk_sb.rearrange("p h (i d) -> p (h i) d", i=2),
                                       table(cos, 2 * (GROUPS + 1)), ALU.mult)
                    pool.tensor_tensor(rope_b[:, :, 0:half], qk_sb[:, :, half:D], table(nsin, GROUPS + 1), ALU.mult)
                    own(pool.tensor_tensor(rope_b[:, :, half:D], qk_sb[:, :, 0:half], table(sin, GROUPS + 1), ALU.mult))
                    if p:
                        filled(pool, g, "krot", p - 1)
                    pool.tensor_tensor(qk_rot, rope_a, rope_b, ALU.add).then_inc(rot_ready, 1)

                def soften(g, p):
                    u = g * CH + p
                    pool.wait_ge(rden_ready, START + u + 1)
                    if p:
                        filled(pool, g, "ksoft", p - 1)
                    pool.tensor_tensor(qk_soft, qk_exp,
                                       rden[:, 0:GROUPS + 1].unsqueeze(2).broadcast_to([P, GROUPS + 1, D]),
                                       ALU.mult).then_inc(soft_ready, 1)

                def fetch_rows(g):
                    pool.wait_ge(rows_added, START + TOP_K * GT * g)
                    pool.tensor_copy(row_slot[:, :, :], slot_out[:, :, bass.ds(g * GT, GT)]).then_inc(slot_ready, 1)
                    pool.wait_ge(slot_ready, START + g + 1)
                    pool.sem_inc(rows_asked, 1)
                    for k in range(TOP_K):
                        for t in range(GT):
                            pool.indirect_dma_start(
                                out=rows[:, k, t, :], out_offset=None, in_=ydisp,
                                in_offset=bass.IndirectOffsetOnAxis(ap=row_slot[:, k, t:t + 1], axis=0))\
                                .then_inc(gathered, 16)

                for counted in (xst_ready, soft_ready, rot_ready, slot_ready, pool_own):
                    pool.sem_inc(counted, START)
                own = Chain(pool, pool_own, START)
                stage(0, 0)
                stage(0, 1)
                for p in range(2):
                    rotate(own, 0, p)
                    soften(0, p)
                first = own.n
                with pool.Fori(0, B * KV) as g:
                    own = Chain(pool, pool_own, START + first + g * CH)
                    for c in range(CH):
                        stage(g, c + 2)
                        rotate(own, g, c + 2)
                        soften(g, c + 2)
                        if c == 1:
                            fetch_rows(g)
                    assert own.n == CH

        s_out = sem("s_out")
        with nc.Block() as block:
            @block.sync
            def _(sp):
                sp.dma_start(out.rearrange("(t p) d -> p t d", p=P), acc[:, :, :]).then_inc(s_out, 16)
                sp.wait_ge(s_out, 16)


def kernel(L0_attn_hidden_states, L0_attn_Wq, L0_attn_Wk, L0_attn_Wv, L0_attn_Wo, L0_ffn_Wg, L0_ffn_w1, L0_ffn_w2):
    import concourse.bacc as bacc
    from concourse.bass_utils import run_bass_kernel_spmd

    def rows_on_partitions(w):
        w = np.asarray(w)
        w = w.reshape(w.shape[:-2] + (w.shape[-2] // P, P, w.shape[-1]))
        return np.ascontiguousarray(np.moveaxis(w, -2, -3))

    def by_head(w, n):
        return rows_on_partitions(w).reshape(P, KC, KV, n).transpose(0, 2, 1, 3)

    const, constb = constants()
    arrays = {
        "x": np.ascontiguousarray(np.asarray(L0_attn_hidden_states).reshape(TOK, HID)),
        "wq": np.ascontiguousarray(by_head(L0_attn_Wq, HD)),
        "wkv": np.ascontiguousarray(np.concatenate([by_head(L0_attn_Wk, D), by_head(L0_attn_Wv, D)], axis=3)),
        "wo": rows_on_partitions(L0_attn_Wo).reshape(P, KV, GROUPS, HID),
        "wg": rows_on_partitions(L0_ffn_Wg),
        "w1": rows_on_partitions(L0_ffn_w1),
        "w2": rows_on_partitions(L0_ffn_w2),
        "const": const,
        "constb": constb.astype(mybir.dt.np(BF16)),
    }
    nc = bacc.Bacc("TRN2", target_bir_lowering=False, num_devices=1)
    ins = [nc.dram_tensor(f"in_{n}", a.shape, mybir.dt.from_np(a.dtype), kind="ExternalInput").ap()
           for n, a in arrays.items()]
    out = nc.dram_tensor("out", (TOK, HID), F32, kind="ExternalOutput").ap()
    build(nc, *ins, out)
    r = run_bass_kernel_spmd(nc, [{f"in_{n}": a for n, a in arrays.items()}], core_ids=[0])
    return r.results[0]["out"].reshape(B, N, HID)
```

```python
import numpy as np
import concourse.bass as bass
from concourse import mybir
from contextlib import ExitStack

F32 = mybir.dt.float32
F32R = mybir.dt.float32r
BF16 = mybir.dt.bfloat16
I32 = mybir.dt.int32
ALU = mybir.AluOpType
ACT = mybir.ActivationFunctionType
AX = mybir.AxisListType

P = 128
B, N, HID = 2, 1024, 256
H, KV, D = 16, 4, 128
GROUPS = H // KV
HD = GROUPS * D
KC = HID // P
CH = N // P
TILES = B * CH
TOK = B * N
FF, E, TOP_K = 1024, 8, 2
FC = FF // P
CAP = -(-5 * TOK * TOP_K // (4 * E))
ST = CAP // P
SLOTS = E * CAP
HALF = CAP // 2
EPS = 1e-5
GATE_NORM = 16.0
SCALE = float(D) ** -0.5
BIG = 1e30
WIDE = 512
MID = D // 2 - 1
START = 1
EXP_AND_LN = 6
FAR = 8192.0

C_ID, C_CUM, C_STRICT, C_ONES, C_MIN = (P * i for i in range(5))
C_COS = 5 * P
C_SIN = C_COS + CH * (D // 2)
C_NSIN = C_SIN + CH * (D // 2)
C_RANK = C_NSIN + CH * (D // 2)
C_BASE = C_RANK + E
C_ALL = C_BASE + E


def constants():
    j, i = np.arange(P)[:, None], np.arange(P)[None, :]
    c = np.zeros((P, C_ALL), np.float32)
    c[:, C_ID:C_ID + P] = j == i
    c[:, C_CUM:C_CUM + P] = (j <= i) / GATE_NORM
    c[:, C_STRICT:C_STRICT + P] = j < i
    c[:, C_ONES:C_ONES + P] = 1.0
    c[:, C_MIN:C_MIN + P] = np.where(j <= i, 3e38, 0.0)
    inv = (1.0 / np.float32(10000.0) ** (np.arange(0, D, 2, dtype=np.float32) / np.float32(D))).astype(np.float32)
    angle = (np.arange(N, dtype=np.float32)[:, None] * inv[None, :]).reshape(CH, P, D // 2).transpose(1, 0, 2)
    c[:, C_COS:C_SIN] = np.cos(angle).reshape(P, -1)
    c[:, C_SIN:C_NSIN] = np.sin(angle).reshape(P, -1)
    c[:, C_NSIN:C_RANK] = -np.sin(angle).reshape(P, -1)
    c[:, C_RANK:C_BASE] = E - np.arange(E)
    c[:, C_BASE:C_ALL] = CAP * np.arange(E)
    m = np.zeros((P, P + WIDE), np.float32)
    m[:, 0:P] = j == i
    m[:, WIDE:] = np.where(i <= j, 0.0, -BIG)
    return c, m


class Chain:

    def __init__(self, eng, sem, base):
        self.eng, self.sem, self.base, self.n = eng, sem, base, 0

    def __call__(self, ins):
        self.n += 1
        ins.then_inc(self.sem, 1)
        self.eng.wait_ge(self.sem, self.base + self.n)


def build(nc, x, wq, wkv, wo, wg, w1, w2, const, constb, out):
    ctx = ExitStack()
    with ctx:
        def sb(name, shape, dt=F32):
            return ctx.enter_context(nc.sbuf_tensor(name, shape, dt))

        def sem(name):
            return ctx.enter_context(nc.semaphore(name))

        xdisp = nc.dram_tensor("xdisp", [SLOTS, HID], F32).ap()
        ydisp = nc.dram_tensor("ydisp", [SLOTS, HID], F32).ap()

        acc = sb("acc", [P, TILES, HID])
        xnT = sb("xnT", [P, KC, TOK])
        wq_in = sb("wq_in", [P, KC, HD])
        wkv_in = sb("wkv_in", [P, KC, 2 * D])
        wo_in = sb("wo_in", [P, GROUPS, HID])
        wg_sb = sb("wg_sb", [P, KC, E])
        cst = sb("cst", [P, C_ALL])
        cstb = sb("cstb", [P, P + WIDE], BF16)
        gate = sb("gate", [P, TOP_K, TILES])
        slot_in = sb("slot_in", [P, TOP_K, TILES], I32)
        slot_out = sb("slot_out", [P, TOP_K, TILES], I32)
        at = [0, 0, None]

        def carve(memory, size):
            at[:] = [0, size, memory]

        def take(n):
            at[0] += n
            assert at[0] <= at[1], at[0]
            return at[2][:, at[0] - n:at[0]]

        psS = ctx.enter_context(nc.psum_tensor("psS", [P, 2, 1024], F32))
        psR = ctx.enter_context(nc.psum_tensor("psR", [P, 3, 512], F32))
        psO = ctx.enter_context(nc.psum_tensor("psO", [P, 512], F32))
        psM = psR[:, 2, :]

        ident = cst[:, C_ID:C_ID + P]
        cum = cst[:, C_CUM:C_CUM + P]
        rank = cst[:, C_RANK:C_RANK + E].unsqueeze(1).broadcast_to([P, TILES // 2, E])
        ebase = cst[:, C_BASE:C_BASE + E].unsqueeze(1).broadcast_to([P, TILES // 2, E])
        identb = cstb[:, 0:P]

        def causalb(n):
            return cstb[:, P + WIDE - n:P + WIDE]


        s_cst = sem("s_cst")
        s_tables = sem("s_tables")
        s_wg = sem("s_wg")
        weights_in = sem("weights_in")

        def load_weights(sp, g):
            head = bass.ds(g & (KV - 1), 1)
            sp.dma_start(wq_in[:, :, :], wq[:, head, :, :]).then_inc(weights_in, 16)
            sp.dma_start(wkv_in[:, :, :], wkv[:, head, :, :]).then_inc(weights_in, 16)
            sp.dma_start(wo_in[:, :, :], wo[:, head, :, :]).then_inc(weights_in, 16)


        stage = ctx.enter_context(ExitStack())
        xn = stage.enter_context(nc.sbuf_tensor("xn", [P, TILES, HID], F32))
        w1_in = stage.enter_context(nc.sbuf_tensor("w1_in", [P, KC, FF], F32))
        w2_in = stage.enter_context(nc.sbuf_tensor("w2_in", [P, FC, HID], F32))
        ROUTING = 3700
        routing = stage.enter_context(nc.sbuf_tensor("routing", [P, ROUTING], F32))
        carve(xn.rearrange("p t d -> p (t d)"), TILES * HID)
        xd = take(ST * HID).rearrange("p (t d) -> p t d", t=ST)
        take((TILES - 2 * ST) * HID)
        yd = take(ST * HID).rearrange("p (t d) -> p t d", t=ST)
        xd_v = xdisp.rearrange("(e t p) d -> e p t d", e=E, p=P)
        yd_v = ydisp.rearrange("(e t p) d -> e p t d", e=E, p=P)


        def parts(name, shape):
            return [stage.enter_context(nc.sbuf_tensor(f"{name}_{part}", shape, F32R)) for part in ("hi", "lo")]

        w1_hi, w1_lo = parts("w1", [P, KC, FF])
        w2_hi, w2_lo = parts("w2", [P, FC, HID])
        xdT_hi, xdT_lo = parts("xdT", [P, KC, CAP])
        hT_hi, hT_lo = parts("hT", [P, FC, CAP])
        s_w1 = sem("s_w1")
        s_w2 = sem("s_w2")
        s_xd = sem("s_xd")
        s_w1hi = sem("s_w1hi")
        s_w1lo = sem("s_w1lo")

        def w1_upper(act, e):
            act.wait_ge(s_w1, 16 * (e + 1))
            for k in range(KC):
                act.activation(w1_hi[:, k, :], w1_in[:, k, :], ACT.Copy).then_inc(s_w1hi, 1)

        def w1_rest(dve, e):
            for k in range(KC):
                dve.wait_ge(s_w1hi, e * KC + k + 1)
                dve.tensor_tensor(w1_lo[:, k, :], w1_in[:, k, :], w1_hi[:, k, :], ALU.subtract).then_inc(s_w1lo, 1)

        carve(routing, ROUTING)
        zero = take(1024)
        PART = 4
        PARTS = TILES // PART
        stats = take(TILES * 6).rearrange("p (t k) -> p t k", t=TILES)
        mean_var = take(TILES * 2).rearrange("p (t k) -> p t k", t=TILES)
        spread = take(TILES)
        std = take(TILES)
        rstd = take(TILES)
        HT = TILES // 2
        small = [take(TILES * E).rearrange("p (t e) -> p t e", t=TILES) for _ in range(11)]
        tot_a, tot_b = (take(HT * E).rearrange("p (t e) -> p t e", e=E) for _ in range(2))
        carry = take(E).unsqueeze(1)
        rt = take(TILES * 12).rearrange("p (k t) -> p k t", k=12)

        s_xp = [sem(f"s_x_{i}") for i in range(PARTS)]
        s_zero = sem("s_zero")
        s_zfill = sem("s_zfill")
        s_a = sem("s_a")
        s_std = sem("s_std")
        s_var = sem("s_var")
        s_xn = sem("s_xn")
        s_tr = sem("s_tr")
        s_xnT = sem("s_xnT")
        s_lg = sem("s_lg")
        s_dl = sem("s_dl")
        s_pe = sem("s_pe")
        s_mask = sem("s_mask")
        s_pos = sem("s_pos")
        s_slots = sem("s_slots")
        s_scat = sem("s_scat")
        FILLS = SLOTS * HID // (P * 1024)

        with nc.Block() as block:
            @block.sync
            def _(sp):
                for i in range(PARTS):
                    tiles = slice(i * PART, (i + 1) * PART)
                    sp.dma_start(acc[:, tiles, :], x[i * PART * P:(i + 1) * PART * P, :].rearrange("(t p) d -> p t d", p=P))\
                      .then_inc(s_xp[i], 16)
                sp.wait_ge(s_zero, 1)
                for e in range(FILLS):
                    rows = P * 1024 // HID
                    sp.dma_start(xdisp[e * rows:(e + 1) * rows, :].rearrange("(p r) d -> p (r d)", p=P),
                                 zero).then_inc(s_zfill, 16)
                sp.dma_start(w1_in[:, :, :], w1[0]).then_inc(s_w1, 16)
                sp.dma_start(w2_in[:, :, :], w2[0]).then_inc(s_w2, 16)
                sp.wait_ge(s_scat, 16 * TOP_K * TILES)
                sp.dma_start(xd, xd_v[0]).then_inc(s_xd, 16)

            @block.gpsimd
            def _(pool):
                pool.memset(zero, 0.0).then_inc(s_zero, 1)
                for half in range(2):
                    pool.wait_ge(s_slots, half + 1)
                    pool.wait_ge(s_xn, HT // 2 * (half + 1))
                    pool.wait_ge(s_zfill, 16 * FILLS)
                    for k in range(TOP_K):
                        for t in range(half * HT, (half + 1) * HT):
                            pool.indirect_dma_start(
                                out=xdisp, out_offset=bass.IndirectOffsetOnAxis(ap=slot_in[:, k, t:t + 1], axis=0),
                                in_=xn[:, t, :], in_offset=None, bounds_check=SLOTS - 1,
                                oob_is_err=False).then_inc(s_scat, 16)
                pool.wait_ge(s_scat, 16 * TOP_K * TILES)

            @block.scalar
            def _(act):
                act.dma_start(cst[:, C_ID:C_ID + P], const[:, C_ID:C_ID + P]).then_inc(s_cst, 16)
                act.dma_start(wg_sb[:, :, :], wg).then_inc(s_wg, 16)
                act.dma_start(cst[:, C_CUM:C_ALL], const[:, C_CUM:C_ALL]).then_inc(s_tables, 16)
                act.dma_start(cstb[:, :], constb).then_inc(s_tables, 16)

                def root(i):
                    tiles = slice(i * PART, (i + 1) * PART)
                    act.wait_ge(s_var, i + 1)
                    act.activation(std[:, tiles], spread[:, tiles], ACT.Sqrt).then_inc(s_std, 1)

                def columns_of(i):
                    act.wait_ge(s_tr, i + 1)
                    act.activation(xnT[:, :, 2 * i * P:2 * (i + 1) * P],
                                   psR[:, i % 2, :].rearrange("p (k t) -> p k t", k=KC), ACT.Copy).then_inc(s_xnT, 1)

                root(0)
                root(1)
                for i in range(PARTS):
                    for j in range(PART // 2):
                        columns_of(i * PART // 2 + j)
                    if i + 2 < PARTS:
                        root(i + 2)
                act.wait_ge(s_dl, 2)
                act.activation(small[1], small[0], ACT.Exp).then_inc(s_pe, 1)
                w1_upper(act, 0)

            @block.tensor
            def _(pe):
                def logits(i):
                    pe.wait_ge(s_xnT, i + 1)
                    for t in range(2 * i, 2 * i + 2):
                        for k in range(KC):
                            last = pe.matmul(psS[:, t // HT, (t % HT) * E:(t % HT + 1) * E],
                                             xnT[:, k, t * P:(t + 1) * P], wg_sb[:, k, :],
                                             start=k == 0, stop=k == KC - 1)
                    last.then_inc(s_lg, 1)

                def count(half):
                    pe.wait_ge(s_mask, half + 1)
                    pe.wait_ge(s_tables, 32)
                    n = HT * E
                    picked = small[5][:, half * HT:(half + 1) * HT, :].rearrange("p t e -> p (t e)")
                    before, all_of = (psS[:, half, 512 + n * i:512 + n * (i + 1)] for i in range(2))
                    pe.matmul(before, cst[:, C_STRICT:C_STRICT + P], picked, start=True, stop=True)
                    pe.matmul(all_of, cst[:, C_ONES:C_ONES + P], picked, start=True, stop=True).then_inc(s_pos, 1)

                pe.wait_ge(s_cst, 16)
                pe.wait_ge(s_wg, 16)
                for i in range(TILES // 2):
                    pe.wait_ge(s_xn, i + 1)
                    if i >= 2:
                        pe.wait_ge(s_xnT, i - 1)
                    for k in range(KC):
                        for t in range(2):
                            last = pe.transpose(psR[:, i % 2, (k * 2 + t) * P:(k * 2 + t + 1) * P],
                                                xn[:, 2 * i + t, k * P:(k + 1) * P], ident)
                    last.then_inc(s_tr, 1)
                    if i:
                        logits(i - 1)
                    if i == HT // 2 + 1:
                        count(0)
                logits(TILES // 2 - 1)
                count(1)

            @block.vector
            def _(dve):
                ch = Chain(dve, s_a, 0)

                def wide(v):
                    return v.unsqueeze(2).broadcast_to([P, HT, E])

                def spreads(i):
                    dve.wait_ge(s_xp[i], 16)
                    for t in range(i * PART, (i + 1) * PART):
                        last = dve.bn_stats(stats[:, t, :], acc[:, t, :])
                    ch(last)
                    for t in range(i * PART, (i + 1) * PART):
                        last = dve.bn_aggr(mean_var[:, t, :], stats[:, t, :])
                    ch(last)
                    tiles = slice(i * PART, (i + 1) * PART)
                    dve.tensor_scalar(spread[:, tiles], mean_var[:, tiles, 1], EPS, None, ALU.add).then_inc(s_var, 1)

                def normalise(i):
                    tiles = slice(i * PART, (i + 1) * PART)
                    dve.wait_ge(s_std, i + 1)
                    ch(dve.reciprocal(rstd[:, tiles], std[:, tiles]))
                    for t in range(i * PART, (i + 1) * PART):
                        last = dve.tensor_scalar(xn[:, t, :], acc[:, t, :], mean_var[:, t, 0:1], rstd[:, t:t + 1],
                                                 ALU.subtract, ALU.mult)
                        if t % 2:
                            last.then_inc(s_xn, 1)

                def route(half):
                    dve.wait_ge(s_tables, 32)
                    tiles = slice(half * HT, (half + 1) * HT)
                    lg, lg2, eq, oh1, oh2, dl, pexp, slot, kept, tmp = \
                        (small[i][:, tiles, :] for i in (2, 3, 4, 6, 7, 0, 1, 8, 9, 10))
                    m1, t1, m2, t2, den, r, e2 = (rt[:, i, tiles] for i in range(7))
                    dve.wait_ge(s_lg, HT // 2 * (half + 1))
                    ch(dve.tensor_copy(lg, psS[:, half, 0:HT * E].rearrange("p (t e) -> p t e", e=E)))
                    ch(dve.tensor_reduce(m1, lg, AX.X, ALU.max))
                    dve.tensor_tensor(dl, lg, wide(m1), ALU.subtract).then_inc(s_dl, 1)
                    ch(dve.tensor_tensor(eq, lg, wide(m1), ALU.is_equal))
                    ch(dve.tensor_tensor(tmp, eq, rank, ALU.mult))
                    ch(dve.tensor_reduce(t1, tmp, AX.X, ALU.max))
                    ch(dve.tensor_tensor(oh1, tmp, wide(t1), ALU.is_equal))
                    ch(dve.scalar_tensor_tensor(out=lg2, in0=oh1, scalar=-BIG, in1=lg, op0=ALU.mult, op1=ALU.add))
                    ch(dve.tensor_reduce(m2, lg2, AX.X, ALU.max))
                    ch(dve.tensor_tensor(eq, lg2, wide(m2), ALU.is_equal))
                    ch(dve.tensor_tensor(tmp, eq, rank, ALU.mult))
                    ch(dve.tensor_reduce(t2, tmp, AX.X, ALU.max))
                    ch(dve.tensor_tensor(oh2, tmp, wide(t2), ALU.is_equal))
                    dve.tensor_tensor(small[5][:, tiles, :], oh1, oh2, ALU.add).then_inc(s_mask, 1)
                    dve.wait_ge(s_pos, half + 1)
                    in_tile, totals = (psS[:, half, 512 + i * HT * E:512 + (i + 1) * HT * E]
                                       .rearrange("p (t e) -> p t e", e=E) for i in range(2))
                    dve.tensor_copy(tot_a[:, 1:, :], totals[:, 0:HT - 1, :])
                    ch(dve.tensor_copy(tot_a[:, 0:1, :], carry))
                    src, dst, step = tot_a, tot_b, 1
                    while step < HT:
                        dve.tensor_copy(dst[:, 0:step, :], src[:, 0:step, :])
                        ch(dve.tensor_tensor(dst[:, step:, :], src[:, step:, :], src[:, 0:HT - step, :], ALU.add))
                        src, dst, step = dst, src, 2 * step
                    ch(dve.tensor_tensor(slot, in_tile, src, ALU.add))
                    if half == 0:
                        dve.tensor_tensor(carry, totals[:, HT - 1:, :], src[:, HT - 1:, :], ALU.add)
                    ch(dve.tensor_scalar(kept, slot, float(CAP), None, ALU.is_lt))
                    ch(dve.tensor_tensor(slot, slot, ebase, ALU.add))
                    own_slot = [rt[:, 7 + k, tiles] for k in range(TOP_K)]
                    own_kept = [rt[:, 9 + k, tiles] for k in range(TOP_K)]
                    pick = [tmp, eq]
                    pick_kept = [lg2, lg]
                    dve.tensor_tensor(pick[0], slot, oh1, ALU.mult)
                    dve.tensor_tensor(pick[1], slot, oh2, ALU.mult)
                    dve.tensor_tensor(pick_kept[0], kept, oh1, ALU.mult)
                    ch(dve.tensor_tensor(pick_kept[1], kept, oh2, ALU.mult))
                    for k in range(TOP_K):
                        dve.tensor_reduce(own_slot[k], pick[k], AX.X, ALU.add)
                        last = dve.tensor_reduce(own_kept[k], pick_kept[k], AX.X, ALU.add)
                    ch(last)
                    far = [rt[:, k, tiles] for k in range(TOP_K)]
                    for k in range(TOP_K):
                        last = dve.scalar_tensor_tensor(out=far[k], in0=own_kept[k], scalar=-FAR, in1=own_slot[k],
                                                        op0=ALU.mult, op1=ALU.add)
                    ch(last)
                    for k in range(TOP_K):
                        last = dve.tensor_scalar(slot_in[:, k, tiles], far[k], FAR, None, ALU.add)
                    last.then_inc(s_slots, 1)
                    return oh2, pexp, den, r, e2, tmp, t1, own_slot, own_kept

                def gates(half, oh2, pexp, den, r, e2, tmp, t1, own_slot, own_kept):
                    tiles = slice(half * HT, (half + 1) * HT)
                    for k in range(TOP_K):
                        dve.tensor_tensor(slot_out[:, k, tiles], own_slot[k], own_kept[k], ALU.mult)
                    dve.wait_ge(s_pe, 1)
                    dve.tensor_reduce(den, pexp, AX.X, ALU.add)
                    ch(dve.tensor_tensor(tmp, pexp, oh2, ALU.mult))
                    dve.tensor_reduce(e2, tmp, AX.X, ALU.add)
                    ch(dve.reciprocal(r, den))
                    dve.tensor_tensor(gate[:, 0, tiles], own_kept[0], r, ALU.mult)
                    ch(dve.tensor_tensor(t1, own_kept[1], r, ALU.mult))
                    dve.tensor_tensor(gate[:, 1, tiles], t1, e2, ALU.mult)

                ch(dve.memset(carry, 0.0))
                spreads(0)
                normalise(0)
                for i in range(1, PARTS):
                    spreads(i)
                    normalise(i)
                routed = [route(half) for half in range(2)]
                for half in range(2):
                    gates(half, *routed[half])
                w1_rest(dve, 0)

        s_xt = sem("s_xt")
        s_xhi = sem("s_xhi")
        s_xdT = sem("s_xdT")
        s_h = sem("s_h")
        s_hhi = sem("s_hhi")
        s_hT = sem("s_hT")
        s_w2hi = sem("s_w2hi")
        s_w2lo = sem("s_w2lo")
        s_y = sem("s_y")
        s_yd = sem("s_yd")
        s_ys = sem("s_ys")
        XT = 3
        YT = 3

        with nc.Block() as block:
            @block.sync
            def _(sp):
                load_weights(sp, 0)
                with sp.Fori(0, E - 1) as e:
                    sp.wait_ge(s_w1lo, (e + 1) * KC)
                    sp.dma_start(w1_in[:, :, :], w1[bass.ds(e + 1, 1)]).then_inc(s_w1, 16)
                    sp.wait_ge(s_xt, (e + 1) * XT)
                    sp.dma_start(xd, xd_v[bass.ds(e + 1, 1)]).then_inc(s_xd, 16)
                    sp.wait_ge(s_w2lo, (e + 1) * FC)
                    sp.dma_start(w2_in[:, :, :], w2[bass.ds(e + 1, 1)]).then_inc(s_w2, 16)

            @block.tensor
            def _(pe):
                def product(out, upper, rest, upper_in, rest_in, first, last):
                    pe.matmul(out, upper, upper_in, start=first, stop=False)
                    pe.matmul(out, upper, rest_in, start=False, stop=False)
                    return pe.matmul(out, rest, upper_in, start=False, stop=last)

                def turn_rows(e, banks):
                    pe.wait_ge(s_xd, 16 * e + 16)
                    for j in banks:
                        pe.wait_ge(s_xdT, START + e * XT + max(j - 1, 0))
                        for t in range(2 * j, min(2 * j + 2, ST)):
                            for k in range(KC):
                                last = pe.transpose(psR[:, j % 2, ((t % 2) * KC + k) * P:((t % 2) * KC + k + 1) * P],
                                                    xd[:, t, k * P:(k + 1) * P], ident)
                        last.then_inc(s_xt, 1)

                def hidden(e):
                    pe.wait_ge(s_xdT, START + (e + 1) * XT)
                    pe.wait_ge(s_w1lo, (e + 1) * KC)
                    for f in range(FC):
                        for n in range(2):
                            pe.wait_ge(s_hT, START + 2 * e * FC + max(2 * (f - 2) + n + 1, 0))
                            for k in range(KC):
                                last = product(psS[:, f % 2, n * 512:n * 512 + HALF],
                                               w1_hi[:, k, f * P:(f + 1) * P], w1_lo[:, k, f * P:(f + 1) * P],
                                               xdT_hi[:, k, n * HALF:(n + 1) * HALF],
                                               xdT_lo[:, k, n * HALF:(n + 1) * HALF], k == 0, k == KC - 1)
                            last.then_inc(s_h, 1)

                def results(e, banks):
                    pe.wait_ge(s_hT, START + 2 * (e + 1) * FC)
                    pe.wait_ge(s_w2lo, (e + 1) * FC)
                    for j in banks:
                        pe.wait_ge(s_yd, START + e * YT + max(j - 1, 0))
                        bank = (psM, psO)[j % 2]
                        for t in range(2 * j, min(2 * j + 2, ST)):
                            for f in range(FC):
                                last = product(bank[:, (t % 2) * HID:(t % 2 + 1) * HID],
                                               hT_hi[:, f, t * P:(t + 1) * P], hT_lo[:, f, t * P:(t + 1) * P],
                                               w2_hi[:, f, :], w2_lo[:, f, :], f == 0, f == FC - 1)
                        last.then_inc(s_y, 1)

                pe.sem_inc(s_y, START)
                turn_rows(0, range(XT))
                with pe.Fori(0, E - 1) as e:
                    hidden(e)
                    turn_rows(e + 1, range(2))
                    results(e, range(1))
                    turn_rows(e + 1, range(2, XT))
                    results(e, range(1, YT))
                hidden(E - 1)
                results(E - 1, range(YT))

            @block.vector
            def _(dve):
                def columns_of(e):
                    for j in range(XT):
                        nt = min(2, ST - 2 * j)

                        def to(part):
                            return part[:, :, 2 * j * P:(2 * j + nt) * P].rearrange("p k (t n) -> p t k n", n=P)

                        turned = psR[:, j % 2, 0:nt * KC * P].rearrange("p (t k n) -> p t k n", k=KC, n=P)
                        dve.wait_ge(s_xt, e * XT + j + 1)
                        dve.tensor_copy(to(xdT_hi), turned).then_inc(s_xhi, 1)
                        dve.wait_ge(s_xhi, e * XT + j + 1)
                        dve.tensor_tensor(to(xdT_lo), turned, to(xdT_hi), ALU.subtract).then_inc(s_xdT, 1)

                def rests(e):
                    for f in range(FC):
                        for n in range(2):
                            cols = slice(n * HALF, (n + 1) * HALF)
                            dve.wait_ge(s_hhi, 2 * e * FC + 2 * f + n + 1)
                            dve.scalar_tensor_tensor(out=hT_lo[:, f, cols], in0=psS[:, f % 2, n * 512:n * 512 + HALF],
                                                     scalar=0.0, in1=hT_hi[:, f, cols], op0=ALU.max,
                                                     op1=ALU.subtract).then_inc(s_hT, 1)
                        dve.wait_ge(s_w2hi, e * FC + f + 1)
                        dve.tensor_tensor(w2_lo[:, f, :], w2_in[:, f, :], w2_hi[:, f, :], ALU.subtract)\
                           .then_inc(s_w2lo, 1)

                dve.sem_inc(s_xdT, START)
                dve.sem_inc(s_hT, START)
                columns_of(0)
                with dve.Fori(0, E - 1) as e:
                    rests(e)
                    columns_of(e + 1)
                    w1_rest(dve, e + 1)
                rests(E - 1)

            @block.scalar
            def _(act):
                def uppers(e):
                    act.wait_ge(s_y, START + e * YT)
                    for f in range(FC):
                        for n in range(2):
                            act.wait_ge(s_h, 2 * e * FC + 2 * f + n + 1)
                            act.activation(hT_hi[:, f, n * HALF:(n + 1) * HALF],
                                           psS[:, f % 2, n * 512:n * 512 + HALF], ACT.Relu).then_inc(s_hhi, 1)
                        if f == 0:
                            act.wait_ge(s_w2, 16 * (e + 1))
                        act.activation(w2_hi[:, f, :], w2_in[:, f, :], ACT.Copy).then_inc(s_w2hi, 1)

                def store_results(e):
                    act.wait_ge(s_ys, START + 16 * e)
                    for j in range(YT):
                        nt = min(2, ST - 2 * j)
                        act.wait_ge(s_y, START + e * YT + j + 1)
                        act.activation(yd[:, 2 * j:2 * j + nt, :],
                                       (psM, psO[:, :])[j % 2][:, 0:nt * HID].rearrange("p (t d) -> p t d", t=nt),
                                       ACT.Copy).then_inc(s_yd, 1)
                    act.wait_ge(s_yd, START + (e + 1) * YT)
                    act.dma_start(yd_v[bass.ds(e, 1)], yd).then_inc(s_ys, 16)

                act.sem_inc(s_yd, START)
                act.sem_inc(s_ys, START)
                with act.Fori(0, E - 1) as e:
                    uppers(e)
                    w1_upper(act, e + 1)
                    store_results(e)
                uppers(E - 1)
                store_results(E - 1)

        stage.close()

        ARENA = 17300
        arena = sb("arena", [P, ARENA])
        carve(arena, ARENA)
        xst_hi, xst_lo = (sb(f"xst_{part}", [P, 2, KC, P], F32R) for part in ("hi", "lo"))
        qT_hi, qT_lo = (sb(f"qT_{part}", [P, 2, HD], F32R) for part in ("hi", "lo"))
        oT_hi, oT_lo = (sb(f"oT_{part}", [P, HD], F32R) for part in ("hi", "lo"))
        wq_hi, wq_lo = (sb(f"wq_{part}", [P, 2, KC, HD], F32R) for part in ("hi", "lo"))
        wkv_hi, wkv_lo = (sb(f"wkv_{part}", [P, 2, KC, 2 * D], F32R) for part in ("hi", "lo"))
        wo_hi, wo_lo = (sb(f"wo_{part}", [P, 2, GROUPS, HID], F32R) for part in ("hi", "lo"))
        kT_hi, kT_lo = (sb(f"kT_{part}", [P, N + P], F32R) for part in ("hi", "lo"))
        qk_sb = take((GROUPS + 1) * D).rearrange("p (h d) -> p h d", d=D)
        qk_exp = take((GROUPS + 1) * D).rearrange("p (h d) -> p h d", d=D)
        qk_soft = take((GROUPS + 1) * D).rearrange("p (h d) -> p h d", d=D)
        rope_a = take((GROUPS + 1) * D).rearrange("p (h d) -> p h d", d=D)
        rope_b = take((GROUPS + 1) * D).rearrange("p (h d) -> p h d", d=D)
        qk_rot = take((GROUPS + 1) * D).rearrange("p (h d) -> p h d", d=D)
        GT = TILES // (B * KV)
        rows = take(TOP_K * GT * HID).rearrange("p (k t d) -> p k t d", k=TOP_K, t=GT)
        nmx = take(8)
        den = take(8)
        rden = take(8)
        kabs = take(D)
        kex = take(D)
        kln = take(D)
        klog = take(D)
        dec_p = take(P)
        dec_n = take(P)
        edge = take(2 * 8).rearrange("p (s k) -> p s k", s=2)
        v_sb = take(CH * D).rearrange("p (c d) -> p c d", d=D)
        v_first = take(2 * D).rearrange("p (c d) -> p c d", d=D)
        qdT = take(2 * HD).rearrange("p (s n) -> p s n", s=2)
        kdT = take(P)
        kd = take(P)
        am = take(2 * HD).rearrange("p (s n) -> p s n", s=2)
        state = take(2 * D).rearrange("p (s n) -> p s n", s=2)
        state_sum = take(D)
        state_raw = take(D)
        prob = take(2 * N).rearrange("p (s n) -> p s n", s=2)
        hmx = take(GROUPS * 2)
        hden = take(GROUPS * 2)
        hrec = take(GROUPS * 2)
        pT = take(2 * CH * 2 * P).rearrange("p (s c h q) -> p s c h q", s=2, c=CH, h=2)
        ADD_ROWS = 4
        row_slot = sb("row_slot", [P, TOP_K, GT], I32)
        row_gate = take(TOP_K * GT).rearrange("p (k t) -> p k t", k=TOP_K)
        cos = cst[:, C_COS:C_SIN].rearrange("p (c d) -> p c d", c=CH)
        sin = cst[:, C_SIN:C_NSIN].rearrange("p (c d) -> p c d", c=CH)
        nsin = cst[:, C_NSIN:C_RANK].rearrange("p (c d) -> p c d", c=CH)

        xst_upper = sem("xst_upper")
        xst_split = sem("xst_split")
        weights_asked = sem("weights_asked")
        weights_upper = sem("weights_upper")
        weights_split = sem("weights_split")
        max_ready = sem("max_ready")
        k_copied = sem("k_copied")
        q_copied = sem("q_copied")
        v_ready = sem("v_ready")
        kln_ready = sem("kln_ready")
        den_ready = sem("den_ready")
        klog_ready = sem("klog_ready")
        rden_ready = sem("rden_ready")
        soft_ready = sem("soft_ready")
        rot_ready = sem("rot_ready")
        rfill = sem("rfill")
        dec_ready = sem("dec_ready")
        qT_upper = sem("qT_upper")
        kT_upper = sem("kT_upper")
        qT_ready = sem("qT_ready")
        kT_ready = sem("kT_ready")
        qdT_ready = sem("qdT_ready")
        kdT_ready = sem("kdT_ready")
        kd_ready = sem("kd_ready")
        am_ready = sem("am_ready")
        raw_ready = sem("raw_ready")
        state_ready = sem("state_ready")
        first_moved = sem("first_moved")
        scored = sem("scored")
        hmax_ready = sem("hmax_ready")
        exped = sem("exped")
        hrec_ready = sem("hrec_ready")
        scaled = sem("scaled")
        pT_act = sem("pT_act")
        pT_dve = sem("pT_dve")
        pv_done = sem("pv_done")
        oT_upper = sem("oT_upper")
        oT_ready = sem("oT_ready")
        acc_done = sem("acc_done")
        slot_ready = sem("slot_ready")
        rows_asked = sem("rows_asked")
        gathered = sem("gathered")
        row_gate_ready = sem("row_gate_ready")
        rows_added = sem("rows_added")
        s_out = sem("s_out")
        act_own = sem("act_own")
        pool_own = sem("pool_own")
        dve_own = sem("dve_own")

        def turn_list(p):
            return [(what, p) for what in ("cum", "qrot", "krot", "qsoft", "ksoft")]

        def linear_list(p):
            return [("att", p)] + [("kd", p), ("outer", p)] * (p % CH < CH - 1)

        BANKS = 3
        before = [("q", 0), ("kv", 0)] + turn_list(0)[:3] + [("q", 1), ("kv", 1)] + turn_list(0)[3:] + linear_list(0)
        turns = []

        def probs_list(c, h):
            return [("pa", (c - 4) * GROUPS + h)] * (c >= 4) + [("pd", c * GROUPS + h)]

        for c in range(CH):
            turns += [("cum", c + 1)]
            turns += probs_list(c, 0)
            turns += [("qrot", c + 1), ("krot", c + 1)]
            turns += [("qsoft", c + 1), ("ksoft", c + 1)]
            turns += [("out", c - 1)] * (c > 0)
            turns += probs_list(c, 1)
            turns += linear_list(c + 1)[:2]
            turns += [("q", c + 2), ("kv", c + 2)]
            turns += probs_list(c, 2)
            turns += probs_list(c, 3)
            turns += linear_list(c + 1)[2:]
        turns.append(("out", CH - 1))
        R0, RT = len(before), len(turns)
        turns += [None] * (-RT % BANKS)
        READ_BY = {"q": (q_copied, CH), "kv": (v_ready, CH), "cum": (dec_ready, CH), "qrot": (qT_ready, CH),
                   "krot": (kT_ready, CH), "qsoft": (qdT_ready, CH), "ksoft": (kdT_ready, CH), "att": (am_ready, CH),
                   "kd": (kd_ready, CH - 1), "outer": (raw_ready, CH - 1), "pa": (pT_act, 4 * GROUPS),
                   "pd": (pT_dve, CH * GROUPS), "out": (acc_done, CH)}

        def nth(p):
            return p - p // CH

        def place(key):
            return R0 + turns.index(key) if key in turns else before.index(key)

        def bank(*key):
            return psR[:, (place(key) - R0) % BANKS, :]

        def filled(eng, g, *key):
            eng.wait_ge(rfill, START + g * RT + place(key) + 1)

        def tokens(g, p):
            b = ((g + p // CH) >> 2) & (B - 1)
            return xnT[:, :, bass.ds(b * N + (p % CH) * P, P)]

        def columns_of_keys(c):
            return slice(N, N + P) if c % CH == 0 else slice(c * P, (c + 1) * P)

        def values_of(p):
            return v_first[:, p % CH, :] if p % CH < 2 else v_sb[:, p % CH, :]

        with nc.Block() as block:
            @block.sync
            def _(sp):
                with sp.Fori(0, B * KV) as g:
                    sp.wait_ge(weights_split, START + 3 * g + 3)
                    sp.sem_inc(weights_asked, 1)
                    load_weights(sp, g + 1)
                for b in range(B):
                    last = (b + 1) * KV - 1
                    for c in range(CH):
                        sp.wait_ge(rows_added, START + TOP_K * GT * (b * KV + c // GT + 1))
                        sp.wait_ge(acc_done, START + last * CH + c + 1)
                        rows_c = (b * CH + c) * P
                        sp.dma_start(out[rows_c:rows_c + P, :], acc[:, b * CH + c, :]).then_inc(s_out, 16)
                sp.wait_ge(s_out, 16 * TILES)

            @block.tensor
            def _(pe):
                def begin(g, *key):
                    n = place(key) - R0
                    if n < 0:
                        last = [(before[n + R0 - BANKS], 0)] if n + R0 >= BANKS else []
                    elif n >= BANKS:
                        last = [(turns[n - BANKS], 0)]
                    else:
                        m = len(turns) + n - BANKS
                        last = [(before[n + R0 - BANKS], 0), (turns[m] or turns[m - BANKS], 1)]
                    for (what, i), groups_ago in last:
                        read, times = READ_BY[what]
                        count = (nth(i) if what in ("kd", "outer") else i) + 1 - groups_ago * times
                        pe.wait_ge(read, START + g * times + max(count, 0))
                    return bank(*key)

                def project(g, p):
                    slot = (g + p // CH) & 1
                    pe.wait_ge(xst_split, START + g * CH + p + 1)
                    for i, (what, width, upper, rest) in enumerate((("q", HD, wq_hi, wq_lo),
                                                                    ("kv", 2 * D, wkv_hi, wkv_lo))):
                        pe.wait_ge(weights_split, START + 3 * (g + p // CH) + i + 1)
                        r = begin(g, what, p)[:, 0:width]
                        for k in range(KC):
                            for x_part, w_part in ((xst_hi, upper), (xst_hi, rest), (xst_lo, upper)):
                                last = pe.matmul(r, x_part[:, p % 2, k, :],
                                                 w_part[:, bass.ds(slot, 1), k, :].rearrange("p s n -> p (s n)"),
                                                 start=k == 0 and w_part is upper and x_part is xst_hi,
                                                 stop=k == KC - 1 and x_part is xst_lo)
                        last.then_inc(rfill, 1)

                def sum_decays(g, p):
                    u = g * CH + p
                    pe.wait_ge(klog_ready, START + u + 1)
                    r = begin(g, "cum", p)
                    pe.matmul(r[:, 0:P], klog, cum, start=True, stop=True).then_inc(rfill, 1)

                def turn_rotated(g, p):
                    u = g * CH + p
                    pe.wait_ge(rot_ready, START + u + 1)
                    r = begin(g, "qrot", p)
                    for h in range(GROUPS):
                        last = pe.transpose(r[:, h * P:(h + 1) * P], qk_rot[:, h, :], ident)
                    last.then_inc(rfill, 1)
                    r = begin(g, "krot", p)
                    pe.transpose(r[:, 0:P], qk_rot[:, GROUPS, :], ident).then_inc(rfill, 1)

                def turn_soft(g, p):
                    u = g * CH + p
                    pe.wait_ge(soft_ready, START + u + 1)
                    r = begin(g, "qsoft", p)
                    for h in range(GROUPS):
                        last = pe.transpose(r[:, h * P:(h + 1) * P], qk_soft[:, h, :], ident)
                    last.then_inc(rfill, 1)
                    r = begin(g, "ksoft", p)
                    pe.transpose(r[:, 0:P], qk_soft[:, GROUPS, :], ident).then_inc(rfill, 1)

                def linear(g, p):
                    u = g * CH + p
                    pe.wait_ge(kdT_ready, START + u + 1)
                    pe.wait_ge(qdT_ready, START + u + 1)
                    pe.wait_ge(v_ready, START + u + 1)
                    r = begin(g, "att", p)
                    pe.matmul(r, kdT, qdT[:, p % 2, :], start=True, stop=True).then_inc(rfill, 1)
                    if p % CH < CH - 1:
                        r = begin(g, "kd", p)
                        pe.transpose(r[:, 0:P], kdT, ident).then_inc(rfill, 1)

                def outer(g, p):
                    if p % CH < CH - 1:
                        u = g * CH + p
                        pe.wait_ge(kd_ready, START + g * (CH - 1) + nth(p) + 1)
                        r = begin(g, "outer", p)
                        pe.matmul(r[:, 0:D], kd, values_of(p), start=True, stop=True).then_inc(rfill, 1)

                def score(g, c, h):
                    n = c * GROUPS + h
                    if h == 0:
                        pe.wait_ge(qT_ready, START + g * CH + c + 1)
                        pe.wait_ge(kT_ready, START + g * CH + c + 1)
                        if c == 1:
                            pe.wait_ge(first_moved, START + 3 * g + 3)
                    if n >= 2:
                        pe.wait_ge(exped, START + g * CH * GROUPS + n - 1)
                    q = slice(h * P, (h + 1) * P)
                    keys = (c % CH + 1) * P
                    for k0 in range(0, keys, WIDE):
                        k1 = min(k0 + WIDE, keys)
                        k = slice(k0, k1) if c % CH else columns_of_keys(c)
                        r = psS[:, h % 2, k0:k1]
                        pe.matmul(r, qT_hi[:, c % 2, q], kT_hi[:, k], start=True, stop=False)
                        pe.matmul(r, qT_hi[:, c % 2, q], kT_lo[:, k], start=False, stop=False)
                        last = pe.matmul(r, qT_lo[:, c % 2, q], kT_hi[:, k], start=False, stop=k1 < keys)
                    pe.matmul(r, identb, causalb(k1 - k0), start=False, stop=True).then_inc(scored, 1)

                def turn_probs(g, c, h):
                    n = c * GROUPS + h
                    pe.wait_ge(scaled, START + g * CH * GROUPS + n + 1)
                    k0 = 0
                    if c >= 4:
                        r = begin(g, "pa", n - 4 * GROUPS)
                        for kb in range(4):
                            last = pe.transpose(r[:, kb * P:(kb + 1) * P], prob[:, h % 2, kb * P:(kb + 1) * P], ident)
                        last.then_inc(rfill, 1)
                        k0 = 4
                    r = begin(g, "pd", n)
                    for kb in range(k0, c + 1):
                        last = pe.transpose(r[:, (kb - k0) * P:(kb - k0 + 1) * P],
                                            prob[:, h % 2, kb * P:(kb + 1) * P], ident)
                    last.then_inc(rfill, 1)

                def weigh(g, c, j):
                    u = g * CH + c
                    cols = slice(j * 2 * P, (j + 1) * 2 * P)
                    if j == 0:
                        pe.wait_ge(oT_ready, START + u)
                    if c:
                        pe.wait_ge(state_ready, START + g * (CH - 1) + c)
                        pe.matmul(psO[:, cols], state[:, c % 2, :], qdT[:, c % 2, cols], start=True, stop=False)
                    if c >= 4:
                        pe.wait_ge(pT_act, START + g * 4 * GROUPS + (c - 4) * GROUPS + 2 * j + 2)
                    pe.wait_ge(pT_dve, START + u * GROUPS + 2 * j + 2)
                    for kb in range(c + 1):
                        last = pe.matmul(psO[:, cols], values_of(0) if c == 0 else v_sb[:, kb, :],
                                         pT[:, j, kb, :, :].rearrange("p h q -> p (h q)"),
                                         start=c == 0, stop=kb == c)
                    last.then_inc(pv_done, 1)

                def outputs(g, c):
                    pe.wait_ge(oT_ready, START + g * CH + c + 1)
                    pe.wait_ge(weights_split, START + 3 * g + 3)
                    r = begin(g, "out", c)
                    for h in range(GROUPS):
                        for o_part, w_part in ((oT_hi, wo_hi), (oT_hi, wo_lo), (oT_lo, wo_hi)):
                            last = pe.matmul(r[:, 0:HID], o_part[:, h * P:(h + 1) * P],
                                             w_part[:, bass.ds(g & 1, 1), h, :].rearrange("p s n -> p (s n)"),
                                             start=h == 0 and o_part is oT_hi and w_part is wo_hi,
                                             stop=h == GROUPS - 1 and o_part is oT_lo)
                    last.then_inc(rfill, 1)

                for counted in (rfill, scored, pv_done):
                    pe.sem_inc(counted, START)
                project(0, 0)
                sum_decays(0, 0)
                turn_rotated(0, 0)
                project(0, 1)
                turn_soft(0, 0)
                score(0, 0, 0)
                score(0, 0, 1)
                linear(0, 0)
                outer(0, 0)
                with pe.Fori(0, B * KV) as g:
                    for c in range(CH):
                        if c:
                            score(g, c, 1)
                        sum_decays(g, c + 1)
                        if c:
                            weigh(g, c - 1, 1)
                        turn_probs(g, c, 0)
                        turn_rotated(g, c + 1)
                        score(g, c, 2)
                        score(g, c, 3)
                        turn_soft(g, c + 1)
                        if c:
                            outputs(g, c - 1)
                        turn_probs(g, c, 1)
                        score(g, c + 1, 0)
                        linear(g, c + 1)
                        project(g, c + 2)
                        turn_probs(g, c, 2)
                        weigh(g, c, 0)
                        turn_probs(g, c, 3)
                        outer(g, c + 1)
                    weigh(g, CH - 1, 1)
                    score(g, CH, 1)
                    outputs(g, CH - 1)

            @block.scalar
            def _(act):
                def tokens_upper(g, p):
                    act.activation(xst_hi[:, p % 2, :, :], tokens(g, p), ACT.Copy).then_inc(xst_upper, 1)

                def read_qkv(g, p):
                    filled(act, g, "q", p)
                    act.wait_ge(rot_ready, START + g * CH + p)
                    act.wait_ge(klog_ready, START + g * CH + p)
                    act.wait_ge(max_ready, START + g * CH + p)
                    act.activation(qk_sb[:, 0:GROUPS, :].rearrange("p h d -> p (h d)"), bank("q", p), ACT.Copy)\
                       .then_inc(q_copied, 1)
                    filled(act, g, "kv", p)
                    act.activation(qk_sb[:, GROUPS, :], bank("kv", p)[:, 0:D], ACT.Copy).then_inc(k_copied, 1)
                    if p < CH:
                        act.wait_ge(pv_done, START + g * 2 * CH)
                    else:
                        act.wait_ge(first_moved, START + 3 * g + 3)
                    act.activation(values_of(p), bank("kv", p)[:, D:2 * D], ACT.Copy).then_inc(v_ready, 1)

                def soften(g, p, heads):
                    u = g * CH + p
                    act.wait_ge(soft_ready, START + u)
                    act.wait_ge(max_ready, START + u + 1)
                    for h in heads:
                        last = act.activation(qk_exp[:, h, :], qk_sb[:, h, :], ACT.Exp,
                                              bias=nmx[:, h:h + 1], accum_out=den[:, h:h + 1])
                    last.then_inc(den_ready, 1)

                def log_sigmoid(own, g, p):
                    act.wait_ge(k_copied, START + g * CH + p + 1)
                    own(act.activation(kabs, qk_sb[:, GROUPS, :], ACT.Abs))
                    own(act.activation(kex, kabs, ACT.Exp, scale=-1.0))
                    act.activation(kln, kex, ACT.Ln, bias=1.0).then_inc(kln_ready, 1)

                def decays(own, g, p):
                    u = g * CH + p
                    filled(act, g, "cum", p)
                    G, e = bank("cum", p), edge[:, p % 2, :]
                    act.wait_ge(raw_ready, START + g * (CH - 1) + max(nth(p) - 1, 0))
                    if p > 1:
                        act.wait_ge(state_ready, START + g * (CH - 1) + p - 2)
                    act.activation(e[:, 0:1], G[:, MID:MID + 1], ACT.Copy)
                    own(act.activation(e[:, 1:2], G[:, MID:MID + 1], ACT.Copy, scale=-1.0))
                    act.activation(e[:, 2:3], G[:, MID:MID + 1], ACT.Exp)
                    act.activation(e[:, 3:4], G[:, P - 1:P], ACT.Exp, bias=e[:, 1:2])
                    act.wait_ge(qdT_ready, START + u)
                    act.wait_ge(kdT_ready, START + u)
                    act.activation(dec_n, G[:, 0:P], ACT.Exp, scale=-1.0, bias=e[:, 0:1])
                    act.activation(dec_p, G[:, 0:P], ACT.Exp, bias=e[:, 1:2]).then_inc(dec_ready, 1)

                def rotated(g, p):
                    filled(act, g, "qrot", p)
                    act.wait_ge(scored, START + GROUPS * (g * CH + max(p - 1, 0)))
                    act.activation(qT_hi[:, p % 2, :], bank("qrot", p), ACT.Copy, scale=SCALE).then_inc(qT_upper, 1)
                    filled(act, g, "krot", p)
                    if p == CH:
                        act.wait_ge(first_moved, START + 3 * g + 3)
                    act.activation(kT_hi[:, columns_of_keys(p)], bank("krot", p)[:, 0:P], ACT.Copy).then_inc(kT_upper, 1)

                def exps(g, c, h):
                    n = c * GROUPS + h
                    keys = (c % CH + 1) * P
                    act.wait_ge(hmax_ready, START + g * CH * GROUPS + n + 1)
                    if n >= 2:
                        filled(act, g, "pd", n - 2)
                    i = (c % 2) * GROUPS + h
                    act.activation(prob[:, h % 2, 0:keys], psS[:, h % 2, 0:keys], ACT.Exp, bias=hmx[:, i:i + 1],
                                   accum_out=hden[:, i:i + 1]).then_inc(exped, 1)

                def columns(g, c, h):
                    if c >= 4:
                        n = (c - 4) * GROUPS + h
                        filled(act, g, "pa", n)
                        act.wait_ge(pv_done, START + 2 * (g * CH + c - 1) + h // 2 + 1)
                        act.activation(pT[:, h // 2, 0:4, h % 2, :], bank("pa", n).rearrange("p (k q) -> p k q", k=4),
                                       ACT.Copy).then_inc(pT_act, 1)

                def turned_keys(g, p):
                    if p % CH < CH - 1:
                        filled(act, g, "kd", p)
                        act.activation(kd, bank("kd", p)[:, 0:P], ACT.Copy).then_inc(kd_ready, 1)

                def read_out(g, c):
                    act.wait_ge(pv_done, START + 2 * (g * CH + c + 1))
                    act.activation(oT_hi[:, :], psO[:, :], ACT.Copy).then_inc(oT_upper, 1)

                for counted in (xst_upper, k_copied, q_copied, v_ready, kln_ready, den_ready, dec_ready, qT_upper,
                                kT_upper, kd_ready, exped, pT_act, oT_upper, act_own):
                    act.sem_inc(counted, START)
                act.add_instruction(mybir.InstLoadActFuncSet(name=nc.get_next_instruction_name(),
                                                             engine=mybir.EngineType.Activation,
                                                             act_func_set_id=EXP_AND_LN))
                own = Chain(act, act_own, START)
                tokens_upper(0, 0)
                tokens_upper(0, 1)
                for p in range(2):
                    read_qkv(0, p)
                    log_sigmoid(own, 0, p)
                    soften(0, p, range(0, 3))
                    soften(0, p, range(3, GROUPS + 1))
                    if p == 0:
                        decays(own, 0, p)
                        rotated(0, p)
                turned_keys(0, 0)
                exps(0, 0, 0)
                exps(0, 0, 1)
                first = own.n
                with act.Fori(0, B * KV) as g:
                    own = Chain(act, act_own, START + first + g * 3 * CH)
                    for c in range(CH):
                        decays(own, g, c + 1)
                        if c:
                            exps(g, c, 1)
                        columns(g, c, 0)
                        if c:
                            read_out(g, c - 1)
                        rotated(g, c + 1)
                        exps(g, c, 2)
                        tokens_upper(g, c + 2)
                        columns(g, c, 1)
                        exps(g, c, 3)
                        turned_keys(g, c + 1)
                        read_qkv(g, c + 2)
                        exps(g, c + 1, 0)
                        log_sigmoid(own, g, c + 2)
                        columns(g, c, 2)
                        columns(g, c, 3)
                        soften(g, c + 2, range(0, 3))
                        soften(g, c + 2, range(3, GROUPS + 1))
                    read_out(g, CH - 1)
                    exps(g, CH, 1)
                    assert own.n == 3 * CH

            @block.vector
            def _(dve):
                causal_min = cst[:, C_MIN:C_MIN + P].unsqueeze(1).broadcast_to([P, GROUPS, P])

                def tokens_rest(g, p):
                    dve.wait_ge(xst_upper, START + g * CH + p + 1)
                    dve.tensor_tensor(xst_lo[:, p % 2, :, :], tokens(g, p), xst_hi[:, p % 2, :, :],
                                      ALU.subtract).then_inc(xst_split, 1)

                def split_weights(g, i):
                    new, upper, rest = ((wq_in, wq_hi, wq_lo), (wkv_in, wkv_hi, wkv_lo), (wo_in, wo_hi, wo_lo))[i]
                    upper, rest = (w[:, bass.ds(g & 1, 1), :, :].rearrange("p s k n -> p (s k) n") for w in (upper, rest))
                    if i == 0:
                        dve.wait_ge(weights_in, 48 * g + 48)
                    dve.tensor_copy(upper, new[:, :, :]).then_inc(weights_upper, 1)
                    dve.wait_ge(weights_upper, START + 3 * g + i + 1)
                    dve.tensor_tensor(rest, new[:, :, :], upper, ALU.subtract).then_inc(weights_split, 1)

                def queries_rest(g, p):
                    dve.wait_ge(qT_upper, START + g * CH + p + 1)
                    dve.scalar_tensor_tensor(out=qT_lo[:, p % 2, :], in0=bank("qrot", p), scalar=SCALE,
                                             in1=qT_hi[:, p % 2, :], op0=ALU.mult, op1=ALU.subtract).then_inc(qT_ready, 1)

                def keys_rest(g, p):
                    dve.wait_ge(kT_upper, START + g * CH + p + 1)
                    k = columns_of_keys(p)
                    dve.tensor_tensor(kT_lo[:, k], bank("krot", p)[:, 0:P], kT_hi[:, k], ALU.subtract).then_inc(kT_ready, 1)

                def read_out_rest(g, c):
                    dve.wait_ge(oT_upper, START + g * CH + c + 1)
                    dve.tensor_tensor(oT_lo[:, :], psO[:, :], oT_hi[:, :], ALU.subtract).then_inc(oT_ready, 1)

                def channel_max(g, p):
                    dve.wait_ge(k_copied, START + g * CH + p + 1)
                    dve.wait_ge(den_ready, START + 2 * (g * CH + p))
                    dve.tensor_reduce(nmx[:, 0:GROUPS + 1], qk_sb, AX.X, ALU.max, negate=True).then_inc(max_ready, 1)

                def log_decay(g, p):
                    dve.wait_ge(kln_ready, START + g * CH + p + 1)
                    if p:
                        filled(dve, g, "cum", p - 1)
                    dve.scalar_tensor_tensor(out=klog, in0=qk_sb[:, GROUPS, :], scalar=0.0, in1=kln, op0=ALU.min,
                                             op1=ALU.subtract).then_inc(klog_ready, 1)

                def soft_sums(g, p):
                    dve.wait_ge(den_ready, START + 2 * (g * CH + p + 1))
                    dve.wait_ge(soft_ready, START + g * CH + p)
                    dve.reciprocal(rden[:, 0:GROUPS + 1], den[:, 0:GROUPS + 1]).then_inc(rden_ready, 1)

                def start_state(g, p):
                    if p % CH:
                        dve.wait_ge(dec_ready, START + g * CH + p + 1)
                        dve.wait_ge(raw_ready, START + g * (CH - 1) + p)
                        dve.wait_ge(pv_done, START + 2 * (g * CH + p - 1))
                        dve.tensor_scalar(state[:, p % 2, :], state_raw, edge[:, p % 2, 2:3], None, ALU.mult)\
                           .then_inc(state_ready, 1)

                def decayed_queries(g, p):
                    u = g * CH + p
                    dve.wait_ge(dec_ready, START + u + 1)
                    filled(dve, g, "qsoft", p)
                    dve.wait_ge(pv_done, START + 2 * (g * CH + max(p - 1, 0)))
                    dve.tensor_tensor(qdT[:, p % 2, :].rearrange("p (h t) -> p h t", t=P),
                                      bank("qsoft", p).rearrange("p (h t) -> p h t", t=P),
                                      dec_p.unsqueeze(1).broadcast_to([P, GROUPS, P]), ALU.mult).then_inc(qdT_ready, 1)

                def decayed_keys(g, p):
                    dve.wait_ge(dec_ready, START + g * CH + p + 1)
                    filled(dve, g, "ksoft", p)
                    dve.tensor_tensor(kdT, bank("ksoft", p)[:, 0:P], dec_n, ALU.mult).then_inc(kdT_ready, 1)

                def masked(g, p):
                    filled(dve, g, "att", p)
                    dve.tensor_tensor(am[:, p % 2, :].rearrange("p (h t) -> p h t", t=P),
                                      bank("att", p).rearrange("p (h t) -> p h t", t=P), causal_min,
                                      ALU.min).then_inc(am_ready, 1)

                def add_state(own, g, p):
                    if p % CH < CH - 1:
                        filled(dve, g, "outer", p)
                        m = bank("outer", p)[:, 0:D]
                        if p % CH:
                            dve.wait_ge(state_ready, START + g * (CH - 1) + p)
                            own(dve.tensor_tensor(state_sum, m, state[:, p % 2, :], ALU.add))
                            m = state_sum
                        dve.tensor_scalar(state_raw, m, edge[:, p % 2, 3:4], None, ALU.mult).then_inc(raw_ready, 1)

                def head_max(g, c, h):
                    dve.wait_ge(scored, START + (g * CH + c) * GROUPS + h + 1)
                    i = (c % 2) * GROUPS + h
                    dve.tensor_reduce(hmx[:, i:i + 1], psS[:, h % 2, 0:(c % CH + 1) * P], AX.X, ALU.max, negate=True)\
                       .then_inc(hmax_ready, 1)

                def head_sum(g, c, h):
                    dve.wait_ge(exped, START + (g * CH + c) * GROUPS + h + 1)
                    i = (c % 2) * GROUPS + h
                    dve.reciprocal(hrec[:, i:i + 1], hden[:, i:i + 1]).then_inc(hrec_ready, 1)

                def head_scale(g, c, h):
                    i = (c % 2) * GROUPS + h
                    dve.wait_ge(hrec_ready, START + (g * CH + c) * GROUPS + h + 1)
                    pr = prob[:, h % 2, 0:(c + 1) * P]
                    dve.tensor_scalar(pr, pr, hrec[:, i:i + 1], None, ALU.mult).then_inc(scaled, 1)

                def columns(g, c, h):
                    n = c * GROUPS + h
                    filled(dve, g, "pd", n)
                    dve.wait_ge(pv_done, START + (2 * (g * CH + c - 1) + h // 2 + 1 if c else 2 * CH * g))
                    r, k0 = bank("pd", n), 4 if c >= 4 else 0
                    if c > k0:
                        dve.tensor_copy(pT[:, h // 2, k0:c, h % 2, :], r[:, 0:(c - k0) * P].rearrange("p (k q) -> p k q", q=P))
                    dve.wait_ge(am_ready, START + g * CH + c + 1)
                    dve.tensor_tensor(pT[:, h // 2, c, h % 2, :], r[:, (c - k0) * P:(c - k0 + 1) * P],
                                      am[:, c % 2, h * P:(h + 1) * P], ALU.add).then_inc(pT_dve, 1)

                def add_out(g, c):
                    filled(dve, g, "out", c)
                    dve.wait_ge(rows_added, START + TOP_K * GT * g + min(max(c + 1 - ADD_ROWS, 0), TOP_K * GT))
                    dve.wait_ge(acc_done, START + g * CH + c)
                    rows_c = acc[:, bass.ds(((g >> 2) & (B - 1)) * CH + c, 1), :].rearrange("p t d -> p (t d)")
                    dve.scalar_tensor_tensor(out=rows_c, in0=bank("out", c)[:, 0:HID], scalar=0.5, in1=rows_c,
                                             op0=ALU.mult, op1=ALU.add).then_inc(acc_done, 1)

                def add_rows(g, c):
                    if c == ADD_ROWS - 1:
                        dve.tensor_copy(row_gate, gate[:, :, bass.ds(g * GT, GT)]).then_inc(row_gate_ready, 1)
                    if 0 <= c - ADD_ROWS < TOP_K * GT:
                        k, t = divmod(c - ADD_ROWS, GT)
                        if c == ADD_ROWS:
                            dve.wait_ge(row_gate_ready, START + g + 1)
                            dve.wait_ge(gathered, 16 * TOP_K * GT * (g + 1))
                        dve.wait_ge(acc_done, START + g * CH + c)
                        dve.wait_ge(rows_added, START + TOP_K * GT * g + c - ADD_ROWS)
                        rows_t = acc[:, bass.ds(g * GT + t, 1), :].rearrange("p t d -> p (t d)")
                        dve.scalar_tensor_tensor(out=rows_t, in0=rows[:, k, t, :], scalar=row_gate[:, k, t:t + 1],
                                                 in1=rows_t, op0=ALU.mult, op1=ALU.add).then_inc(rows_added, 1)

                def move_first(g):
                    dve.wait_ge(pv_done, START + g * 2 * CH)
                    dve.wait_ge(v_ready, START + g * CH + 2)
                    dve.tensor_copy(v_sb[:, 0:2, :], v_first).then_inc(first_moved, 1)
                    dve.wait_ge(kT_ready, START + g * CH + 1)
                    first = columns_of_keys(0)
                    dve.tensor_copy(kT_hi[:, 0:P], kT_hi[:, first]).then_inc(first_moved, 1)
                    dve.tensor_copy(kT_lo[:, 0:P], kT_lo[:, first]).then_inc(first_moved, 1)

                for counted in (qT_ready, kT_ready, oT_ready, xst_split, weights_upper, weights_split, max_ready,
                                first_moved, klog_ready, rden_ready, qdT_ready, kdT_ready, am_ready,
                                raw_ready, state_ready, hmax_ready, hrec_ready, scaled, pT_dve, acc_done,
                                row_gate_ready, rows_added, dve_own):
                    dve.sem_inc(counted, START)
                own = Chain(dve, dve_own, START)
                split_weights(0, 0)
                tokens_rest(0, 0)
                split_weights(0, 1)
                tokens_rest(0, 1)
                channel_max(0, 0)
                log_decay(0, 0)
                soft_sums(0, 0)
                queries_rest(0, 0)
                keys_rest(0, 0)
                decayed_queries(0, 0)
                decayed_keys(0, 0)
                channel_max(0, 1)
                log_decay(0, 1)
                split_weights(0, 2)
                masked(0, 0)
                add_state(own, 0, 0)
                head_max(0, 0, 0)
                head_max(0, 0, 1)
                assert own.n == 0
                with dve.Fori(0, B * KV) as g:
                    own = Chain(dve, dve_own, START + g * (CH - 2))
                    for c in range(CH):
                        head_sum(g, c, 0)
                        head_scale(g, c, 0)
                        if c:
                            head_max(g, c, 1)
                        soft_sums(g, c + 1)
                        columns(g, c, 0)
                        if c == 0:
                            move_first(g)
                        head_sum(g, c, 1)
                        if c:
                            read_out_rest(g, c - 1)
                        queries_rest(g, c + 1)
                        keys_rest(g, c + 1)
                        head_max(g, c, 2)
                        head_scale(g, c, 1)
                        decayed_queries(g, c + 1)
                        decayed_keys(g, c + 1)
                        head_max(g, c, 3)
                        if c:
                            add_out(g, c - 1)
                        tokens_rest(g, c + 2)
                        columns(g, c, 1)
                        head_sum(g, c, 2)
                        head_max(g, c + 1, 0)
                        masked(g, c + 1)
                        head_sum(g, c, 3)
                        head_scale(g, c, 2)
                        if 2 <= c < 5:
                            split_weights(g + 1, c - 2)
                        channel_max(g, c + 2)
                        start_state(g, c + 1)
                        head_scale(g, c, 3)
                        columns(g, c, 2)
                        log_decay(g, c + 2)
                        add_rows(g, c)
                        columns(g, c, 3)
                        add_state(own, g, c + 1)
                    read_out_rest(g, CH - 1)
                    head_max(g, CH, 1)
                    add_out(g, CH - 1)
                    assert own.n == CH - 2

            @block.gpsimd
            def _(pool):
                half = D // 2

                def rotate(own, g, p):
                    u = g * CH + p

                    def table(t, n):
                        return t[:, p % CH, :].unsqueeze(1).broadcast_to([P, n, half])

                    pool.wait_ge(k_copied, START + u + 1)
                    pool.wait_ge(q_copied, START + u + 1)
                    pool.tensor_tensor(rope_a.rearrange("p h (i d) -> p (h i) d", i=2),
                                       qk_sb.rearrange("p h (i d) -> p (h i) d", i=2),
                                       table(cos, 2 * (GROUPS + 1)), ALU.mult)
                    pool.tensor_tensor(rope_b[:, :, 0:half], qk_sb[:, :, half:D], table(nsin, GROUPS + 1), ALU.mult)
                    own(pool.tensor_tensor(rope_b[:, :, half:D], qk_sb[:, :, 0:half], table(sin, GROUPS + 1), ALU.mult))
                    if p:
                        filled(pool, g, "krot", p - 1)
                    pool.tensor_tensor(qk_rot, rope_a, rope_b, ALU.add).then_inc(rot_ready, 1)

                def soften(g, p):
                    u = g * CH + p
                    pool.wait_ge(rden_ready, START + u + 1)
                    if p:
                        filled(pool, g, "ksoft", p - 1)
                    pool.tensor_tensor(qk_soft, qk_exp,
                                       rden[:, 0:GROUPS + 1].unsqueeze(2).broadcast_to([P, GROUPS + 1, D]),
                                       ALU.mult).then_inc(soft_ready, 1)

                def fetch_rows(g):
                    pool.wait_ge(rows_added, START + TOP_K * GT * g)
                    pool.tensor_copy(row_slot[:, :, :], slot_out[:, :, bass.ds(g * GT, GT)]).then_inc(slot_ready, 1)
                    pool.wait_ge(slot_ready, START + g + 1)
                    pool.sem_inc(rows_asked, 1)
                    for k in range(TOP_K):
                        for t in range(GT):
                            pool.indirect_dma_start(
                                out=rows[:, k, t, :], out_offset=None, in_=ydisp,
                                in_offset=bass.IndirectOffsetOnAxis(ap=row_slot[:, k, t:t + 1], axis=0))\
                                .then_inc(gathered, 16)

                for counted in (soft_ready, rot_ready, slot_ready, pool_own):
                    pool.sem_inc(counted, START)
                own = Chain(pool, pool_own, START)
                pool.wait_ge(s_ys, START + 16 * E)
                for p in range(2):
                    rotate(own, 0, p)
                    if p == 0:
                        soften(0, p)
                first = own.n
                with pool.Fori(0, B * KV) as g:
                    own = Chain(pool, pool_own, START + first + g * CH)
                    for c in range(CH):
                        soften(g, c + 1)
                        if c == ADD_ROWS - 1:
                            fetch_rows(g)
                        rotate(own, g, c + 2)
                    assert own.n == CH


def kernel(L0_attn_hidden_states, L0_attn_Wq, L0_attn_Wk, L0_attn_Wv, L0_attn_Wo, L0_ffn_Wg, L0_ffn_w1, L0_ffn_w2):
    import concourse.bacc as bacc
    from concourse.bass_utils import run_bass_kernel_spmd

    def rows_on_partitions(w):
        w = np.asarray(w)
        w = w.reshape(w.shape[:-2] + (w.shape[-2] // P, P, w.shape[-1]))
        return np.ascontiguousarray(np.moveaxis(w, -2, -3))

    def by_head(w, n):
        return rows_on_partitions(w).reshape(P, KC, KV, n).transpose(0, 2, 1, 3)

    const, constb = constants()
    arrays = {
        "x": np.ascontiguousarray(np.asarray(L0_attn_hidden_states).reshape(TOK, HID)),
        "wq": np.ascontiguousarray(by_head(L0_attn_Wq, HD)),
        "wkv": np.ascontiguousarray(np.concatenate([by_head(L0_attn_Wk, D), by_head(L0_attn_Wv, D)], axis=3)),
        "wo": rows_on_partitions(L0_attn_Wo).reshape(P, KV, GROUPS, HID),
        "wg": rows_on_partitions(L0_ffn_Wg),
        "w1": rows_on_partitions(L0_ffn_w1),
        "w2": rows_on_partitions(L0_ffn_w2),
        "const": const,
        "constb": constb.astype(mybir.dt.np(BF16)),
    }
    nc = bacc.Bacc("TRN2", target_bir_lowering=False, num_devices=1)
    ins = [nc.dram_tensor(f"in_{n}", a.shape, mybir.dt.from_np(a.dtype), kind="ExternalInput").ap()
           for n, a in arrays.items()]
    out = nc.dram_tensor("out", (TOK, HID), F32, kind="ExternalOutput").ap()
    build(nc, *ins, out)
    r = run_bass_kernel_spmd(nc, [{f"in_{n}": a for n, a in arrays.items()}], core_ids=[0])
    return r.results[0]["out"].reshape(B, N, HID)
```
